# Optimizing a Trainium2 kernel written in Bass

```python
import numpy as np
import jax
import jax.numpy as jnp

def _softmax(x, axis=-1):
    return jax.nn.softmax(x, axis=axis)

def _gelu(x):
    return jax.nn.gelu(x, approximate=True)

def _silu(x):
    return jax.nn.silu(x)

def _sigmoid(x):
    return jax.nn.sigmoid(x)

def _layernorm(x, axis=-1, eps=1e-05):
    m = jnp.mean(x, axis=axis, keepdims=True)
    v = jnp.var(x, axis=axis, keepdims=True)
    return (x - m) / jnp.sqrt(v + eps)

def _scatter_add(tgt, idx, src, axis=0):
    return tgt.at[idx].add(src)

def _segment_sum(src, seg, n):
    return jax.ops.segment_sum(src, seg, n)
kernel_name = 'mk_adaln_attn_ffn_d1_seqx_r8_ce030b'

def setup_inputs(seed: int=0):
    np.random.seed(seed)
    _w = jnp.asarray

    def _rec_inputs():
        import jax
        import jax.numpy as jnp
        _rk = jax.random.key(seed)
        x = -0.000125 + 0.9999 * jax.random.normal(jax.random.fold_in(_rk, 1), (8, 256, 128), jnp.float32)
        _lenS = 256 - jax.random.randint(jax.random.fold_in(_rk, 7), (8,), 0, max(1, 256 // 4) + 1, jnp.int32)
        _lenS2 = 256 - jax.random.randint(jax.random.fold_in(_rk, 8), (8,), 0, max(1, 256 // 4) + 1, jnp.int32)
        condB_deltat = jax.random.uniform(jax.random.fold_in(_rk, 11), (8,), jnp.float32, 0.0, 1.99976)
        itok_B_0_15 = jax.random.randint(jax.random.fold_in(_rk, 12), (8,), 0, 16, jnp.int32)
        return (x, condB_deltat, itok_B_0_15)
    x, condB_deltat, itok_B_0_15 = _rec_inputs()

    def _L0_cond_setup():
        import jax, jax.numpy as jnp
        import numpy as np
        B, F, T = (32, 64, 128)
        key = jax.random.key(seed)
        k1, k2, k3, k4 = jax.random.split(key, 4)
        x = jax.random.normal(k1, (B, 2 * F, T), dtype=jnp.float32)
        delta_t = jax.random.uniform(k2, (B,), dtype=jnp.float32, minval=0.5, maxval=2.0)
        amplitudes = jax.random.uniform(k3, (F,), dtype=jnp.float32, minval=0.7, maxval=1.3)
        frequencies = jax.random.uniform(k4, (F,), dtype=jnp.float32, minval=0.0, maxval=2.0 * np.pi)
        return {'x': x, 'delta_t': delta_t, 'amplitudes': amplitudes, 'frequencies': frequencies}
    _L0_cond_all = _L0_cond_setup()
    _L0_cond_in = {k: v for k, v in _L0_cond_all.items() if k in ('amplitudes', 'frequencies')}
    del _L0_cond_all

    def _L0_attn_setup():
        import jax, jax.numpy as jnp
        import numpy as np
        DECAY = 0.95
        EPS = 1e-05
        B, T, D, L = (4, 512, 128, 2)

        def _layer_norm(x, w, b):
            mu = jnp.mean(x, axis=-1, keepdims=True)
            var = jnp.mean(jnp.square(x - mu), axis=-1, keepdims=True)
            return (x - mu) * jax.lax.rsqrt(var + EPS) * w + b

        def _time_mix_layer(x, ln_w, ln_b, Wk, Wv, Wr, Wo):
            normed = _layer_norm(x, ln_w, ln_b)
            k = jnp.einsum('btd,ed->bte', normed, Wk)
            v = jnp.einsum('btd,ed->bte', normed, Wv)
            r = jax.nn.sigmoid(jnp.einsum('btd,ed->bte', normed, Wr))
            kv = k * v

            def step(state, kv_t):
                state = DECAY * state + (1.0 - DECAY) * kv_t
                return (state, state)
            init = jnp.zeros((x.shape[0], x.shape[2]), dtype=x.dtype)
            _, states = jax.lax.scan(step, init, jnp.swapaxes(kv, 0, 1))
            y = r * jnp.swapaxes(states, 0, 1)
            y = jnp.einsum('btd,ed->bte', y, Wo)
            return x + y
        key = jax.random.key(seed)
        ks = jax.random.split(key, 7)
        scale = 1.0 / np.sqrt(D)
        return {'h': jax.random.normal(ks[0], (B, T, D), dtype=jnp.float32), 'ln_w': jnp.ones((L, D), dtype=jnp.float32), 'ln_b': jnp.zeros((L, D), dtype=jnp.float32), 'Wk': jax.random.normal(ks[1], (L, D, D), dtype=jnp.float32) * scale, 'Wv': jax.random.normal(ks[2], (L, D, D), dtype=jnp.float32) * scale, 'Wr': jax.random.normal(ks[3], (L, D, D), dtype=jnp.float32) * scale, 'Wo': jax.random.normal(ks[4], (L, D, D), dtype=jnp.float32) * scale}
    _L0_attn_all = _L0_attn_setup()
    _L0_attn_in = {k: v for k, v in _L0_attn_all.items() if k in ('ln_w', 'ln_b', 'Wk', 'Wv', 'Wr', 'Wo')}
    del _L0_attn_all

    def _L0_cond2_setup():
        import jax, jax.numpy as jnp
        import numpy as np
        INPUT_DIM = 128
        OUTPUT_DIM = 128
        NUM_CATEGORIES = 16
        B, S = (32, 64)
        key = jax.random.key(seed)
        kx, kw, kb, ki = jax.random.split(key, 4)
        k = 1.0 / np.sqrt(INPUT_DIM)
        x = jax.random.normal(kx, (B, S, INPUT_DIM), dtype=jnp.float32)
        weight = jax.random.uniform(kw, (NUM_CATEGORIES, INPUT_DIM, OUTPUT_DIM), dtype=jnp.float32, minval=-k, maxval=k)
        bias = jax.random.uniform(kb, (NUM_CATEGORIES, OUTPUT_DIM), dtype=jnp.float32, minval=-k, maxval=k)
        emb_ids = jax.random.randint(ki, (B,), 0, NUM_CATEGORIES, dtype=jnp.int64)
        return {'x': x, 'emb_ids': emb_ids, 'weight': weight, 'bias': bias}
    _L0_cond2_all = _L0_cond2_setup()
    _L0_cond2_in = {k: v for k, v in _L0_cond2_all.items() if k in ('weight', 'bias')}
    del _L0_cond2_all

    def _L0_ffn_setup():
        import jax, jax.numpy as jnp
        import numpy as np
        B, S, M, E, DFF = (4, 256, 128, 8, 512)
        CAPACITY_FACTOR = 1.25

        def _top1_gate(tokens, wg, capacity):
            gates = jax.nn.softmax(tokens @ wg)
            expert_idx = jnp.argmax(gates, axis=-1)
            mask1 = jax.nn.one_hot(expert_idx, gates.shape[-1], dtype=gates.dtype)
            pos = jnp.sum(jnp.cumsum(mask1, axis=0) * mask1, axis=-1).astype(jnp.int32) - 1
            keep = (pos < capacity).astype(gates.dtype)
            mask1c = mask1 * keep[:, None]
            gates1 = jnp.sum(gates * mask1c, axis=-1)
            loc_oh = jax.nn.one_hot(pos, capacity, dtype=gates.dtype)
            combine = gates1[:, None, None] * mask1c[:, :, None] * loc_oh[:, None, :]
            dispatch = (combine > 0).astype(tokens.dtype)
            return (combine, dispatch)
        key = jax.random.key(seed)
        k = jax.random.split(key, 5)
        x = jax.random.normal(k[0], (B, S, M), dtype=jnp.float32)
        wg = jax.random.normal(k[1], (M, E), dtype=jnp.float32) * 0.02
        w1 = jax.random.normal(k[2], (E, M, DFF), dtype=jnp.float32) * 0.02
        b1 = jnp.zeros((E, DFF), dtype=jnp.float32)
        w2 = jax.random.normal(k[3], (E, DFF, M), dtype=jnp.float32) * 0.02
        b2 = jnp.zeros((E, M), dtype=jnp.float32)
        return {'x': x, 'wg': wg, 'w1': w1, 'b1': b1, 'w2': w2, 'b2': b2}
    _L0_ffn_all = _L0_ffn_setup()
    _L0_ffn_in = {k: v for k, v in _L0_ffn_all.items() if k in ('wg', 'w1', 'b1', 'w2', 'b2')}
    del _L0_ffn_all
    return {'x': x, 'condB_deltat': condB_deltat, 'itok_B_0_15': itok_B_0_15, 'L0_cond_amplitudes': _L0_cond_in['amplitudes'], 'L0_cond_frequencies': _L0_cond_in['frequencies'], 'L0_attn_ln_w': _L0_attn_in['ln_w'], 'L0_attn_ln_b': _L0_attn_in['ln_b'], 'L0_attn_Wk': _L0_attn_in['Wk'], 'L0_attn_Wv': _L0_attn_in['Wv'], 'L0_attn_Wr': _L0_attn_in['Wr'], 'L0_attn_Wo': _L0_attn_in['Wo'], 'L0_cond2_weight': _L0_cond2_in['weight'], 'L0_cond2_bias': _L0_cond2_in['bias'], 'L0_ffn_wg': _L0_ffn_in['wg'], 'L0_ffn_w1': _L0_ffn_in['w1'], 'L0_ffn_b1': _L0_ffn_in['b1'], 'L0_ffn_w2': _L0_ffn_in['w2'], 'L0_ffn_b2': _L0_ffn_in['b2']}

def reference(x, condB_deltat, itok_B_0_15, L0_cond_amplitudes, L0_cond_frequencies, L0_attn_ln_w, L0_attn_ln_b, L0_attn_Wk, L0_attn_Wv, L0_attn_Wr, L0_attn_Wo, L0_cond2_weight, L0_cond2_bias, L0_ffn_wg, L0_ffn_w1, L0_ffn_b1, L0_ffn_w2, L0_ffn_b2):
    import jax
    import jax.numpy as jnp

    def _L0_cond_ref(x, delta_t, amplitudes, frequencies):
        import jax, jax.numpy as jnp
        import numpy as np
        B, F, T = (32, 64, 128)
        Bn = x.shape[0]
        Fn = amplitudes.shape[0]
        a = amplitudes[None, :] ** delta_t[:, None]
        ang = frequencies[None, :] * delta_t[:, None]
        c = a * jnp.cos(ang)
        s = a * jnp.sin(ang)
        xr = x.reshape(Bn, Fn, 2, -1)
        x0, x1 = (xr[:, :, 0], xr[:, :, 1])
        out0 = c[..., None] * x0 - s[..., None] * x1
        out1 = s[..., None] * x0 + c[..., None] * x1
        return jnp.stack([out0, out1], axis=2).reshape(x.shape)

    def _L0_attn_ref(h, ln_w, ln_b, Wk, Wv, Wr, Wo):
        import jax, jax.numpy as jnp
        import numpy as np
        DECAY = 0.95
        EPS = 1e-05
        B, T, D, L = (4, 512, 128, 2)

        def _layer_norm(x, w, b):
            mu = jnp.mean(x, axis=-1, keepdims=True)
            var = jnp.mean(jnp.square(x - mu), axis=-1, keepdims=True)
            return (x - mu) * jax.lax.rsqrt(var + EPS) * w + b

        def _time_mix_layer(x, ln_w, ln_b, Wk, Wv, Wr, Wo):
            normed = _layer_norm(x, ln_w, ln_b)
            k = jnp.einsum('btd,ed->bte', normed, Wk)
            v = jnp.einsum('btd,ed->bte', normed, Wv)
            r = jax.nn.sigmoid(jnp.einsum('btd,ed->bte', normed, Wr))
            kv = k * v

            def step(state, kv_t):
                state = DECAY * state + (1.0 - DECAY) * kv_t
                return (state, state)
            init = jnp.zeros((x.shape[0], x.shape[2]), dtype=x.dtype)
            _, states = jax.lax.scan(step, init, jnp.swapaxes(kv, 0, 1))
            y = r * jnp.swapaxes(states, 0, 1)
            y = jnp.einsum('btd,ed->bte', y, Wo)
            return x + y
        out = h
        for i in range(Wk.shape[0]):
            out = _time_mix_layer(out, ln_w[i], ln_b[i], Wk[i], Wv[i], Wr[i], Wo[i])
        return out

    def _L0_cond2_ref(x, emb_ids, weight, bias):
        import jax, jax.numpy as jnp
        import numpy as np
        INPUT_DIM = 128
        OUTPUT_DIM = 128
        NUM_CATEGORIES = 16
        B, S = (32, 64)
        ids = emb_ids.reshape(-1).astype(jnp.int32)
        w = weight[ids]
        b = bias[ids]
        return jnp.einsum('bsi,bij->bsj', x, w) + b[:, None, :]

    def _L0_ffn_ref(x, wg, w1, b1, w2, b2):
        import jax, jax.numpy as jnp
        import numpy as np
        B, S, M, E, DFF = (4, 256, 128, 8, 512)
        CAPACITY_FACTOR = 1.25

        def _top1_gate(tokens, wg, capacity):
            gates = jax.nn.softmax(tokens @ wg)
            expert_idx = jnp.argmax(gates, axis=-1)
            mask1 = jax.nn.one_hot(expert_idx, gates.shape[-1], dtype=gates.dtype)
            pos = jnp.sum(jnp.cumsum(mask1, axis=0) * mask1, axis=-1).astype(jnp.int32) - 1
            keep = (pos < capacity).astype(gates.dtype)
            mask1c = mask1 * keep[:, None]
            gates1 = jnp.sum(gates * mask1c, axis=-1)
            loc_oh = jax.nn.one_hot(pos, capacity, dtype=gates.dtype)
            combine = gates1[:, None, None] * mask1c[:, :, None] * loc_oh[:, None, :]
            dispatch = (combine > 0).astype(tokens.dtype)
            return (combine, dispatch)
        d_model = x.shape[-1]
        tokens = x.reshape(-1, d_model)
        T = tokens.shape[0]
        num_experts = wg.shape[1]
        capacity = int(CAPACITY_FACTOR * T / num_experts)
        combine, dispatch = _top1_gate(tokens, wg, capacity)
        dispatched = jnp.einsum('sec,sm->ecm', dispatch, tokens)
        h = jax.nn.relu(jnp.einsum('ecm,emf->ecf', dispatched, w1) + b1[:, None, :])
        expert_out = jnp.einsum('ecf,efm->ecm', h, w2) + b2[:, None, :]
        combined = jnp.einsum('sec,ecm->sm', combine, expert_out)
        return combined.reshape(x.shape)
    x = x + _L0_attn_ref(_L0_cond_ref(x, condB_deltat, L0_cond_amplitudes, L0_cond_frequencies), L0_attn_ln_w, L0_attn_ln_b, L0_attn_Wk, L0_attn_Wv, L0_attn_Wr, L0_attn_Wo)
    x = x + _L0_ffn_ref(_L0_cond2_ref(x, itok_B_0_15, L0_cond2_weight, L0_cond2_bias), L0_ffn_wg, L0_ffn_w1, L0_ffn_b1, L0_ffn_w2, L0_ffn_b2)
    return x

_drawn_inputs = setup_inputs


def setup_inputs(seed=0):
    import zlib

    import numpy as np

    out = dict(_drawn_inputs(seed))
    spreads = {'L0_attn_ln_w': (1.0, 0.2),
     'L0_attn_ln_b': (0.0, 0.51),
     'L0_ffn_b1': (0.0, 0.8),
     'L0_ffn_b2': (0.0, 0.759)}
    factors = {'L0_cond2_weight': 4.462,
     'L0_cond2_bias': 8.0,
     'L0_ffn_wg': 4.47,
     'L0_ffn_w1': 8.0,
     'L0_ffn_w2': 6.937}
    for name, (base, spread) in spreads.items():
        noise = np.random.default_rng([zlib.crc32(name.encode()), seed]).standard_normal(out[name].shape)
        drawn = base * np.exp(spread * noise) if base else spread * noise
        out[name] = jnp.asarray(drawn.astype(out[name].dtype))
    for name, factor in factors.items():
        out[name] = (out[name] * factor).astype(out[name].dtype)
    return out
```

```python
from contextlib import ExitStack

import concourse.bass as bass
from concourse import mybir

ALU = mybir.AluOpType
ACT = mybir.ActivationFunctionType
AX_X = mybir.AxisListType.X
F32 = mybir.dt.float32
BF16 = mybir.dt.bfloat16
I32 = mybir.dt.int32

B, S, D = 8, 256, 128
J = 4
Q = 4
BT = B * S // Q
NL = 2
E, DFF = 8, 512
FC = DFF // D
NCAT = 16
NTOK = B * S
CAP = int(1.25 * NTOK / E)
SLOTS = E * CAP
PAIRS = E // 2
PC = 2 * CAP // 128
ROW = 2 * D + 2
GATE, TOK = 2 * D, 2 * D + 1
NOBODY = 1 << 20
DECAY = 0.95
EPS = 1e-5
NSTEP = Q * NL

P_LNW, P_LNB, P_B1, P_B2, P_BIAS = 0, NL, 2 * NL, 2 * NL + E * FC, 2 * NL + E * FC + E
NPAR = P_BIAS + NCAT
R_DT, R_AMP, R_FREQ = 0, Q, Q + 1
NROT = Q + 2

TWO_PI = 6.283185307179586
C1 = 6.28125
C2 = 0.0019340515136718750
C3 = TWO_PI - C1 - C2
PI_IN = 3.1415925
ROUND = 12582912.0


def build(nc, x, rot_par, itok, params, wqkv, w_cat, wg, w1, w2, out):
    ctx = ExitStack()
    with ctx:
        def sb(name, shape, dt=F32):
            return ctx.enter_context(nc.sbuf_tensor(name, shape, dt))

        def sem(name):
            return ctx.enter_context(nc.semaphore(name))

        slots = nc.dram_tensor("slots", (SLOTS + NTOK, ROW), F32).ap()

        xt = sb("xt", [128, Q, BT])
        rot = sb("rot", [128, NROT])
        par = sb("par", [128, NPAR])
        tok_id = sb("tok_id", [128, B], I32)
        wt = sb("wt", [128, NL, 4, D])
        wcat = sb("wcat", [128, B, D])
        wg_sb = sb("wg_sb", [128, E])
        w1_sb = sb("w1_sb", [128, E, DFF])
        w2_sb = sb("w2_sb", [128, E, FC, D])

        identf = sb("identf", [128, 128])
        before = sb("before", [128, 128], BF16)
        upto = sb("upto", [128, 128], BF16)
        onesb = sb("onesb", [128, 128], BF16)
        decay = sb("decay", [128, BT])
        empty = sb("empty", [128, ROW])
        mhalf = sb("mhalf", [128, J])
        rank = sb("rank", [128, J, E])
        ranki = sb("ranki", [128, J, E], I32)
        trashi = sb("trashi", [128, Q, J], I32)
        trash = sb("trash", [128, Q, J])
        cati = sb("cati", [128, B, NCAT], I32)
        catf = sb("catf", [128, B, NCAT])
        rowi = sb("rowi", [128, 1], I32)
        rowf = sb("rowf", [128, 1])
        idf = sb("idf", [128, B])
        wrow = sb("wrow", [128, B], I32)
        cat_hot = sb("cat_hot", [128, B, NCAT])
        cat_sel = sb("cat_sel", [128, B, NCAT])
        bias = sb("bias", [128, B])

        ang = sb("ang", [128, Q])
        turns = sb("turns", [128, 2, Q])
        red = sb("red", [128, 4, Q])
        sins = sb("sins", [128, 2, Q])
        cosr = sb("cosr", [128, 2, Q])
        amp = sb("amp", [128, Q])
        ac = sb("ac", [128, Q])
        asn = sb("asn", [128, Q])
        sx = sb("sx", [128, Q, BT])
        h = sb("h", [128, Q, J, D])
        xh = sb("xh", [128, Q, J, D])
        stats = sb("stats", [128, NSTEP, J, 6])
        mv = sb("mv", [128, NSTEP, J, 2])
        veps = sb("veps", [128, NSTEP, J])
        rstd = sb("rstd", [128, NSTEP, J])
        nrm = sb("nrm", [128, 2, J, D])
        xn = sb("xn", [128, 2, BT])
        vs = sb("vs", [128, 2, BT])
        th = sb("th", [128, 2, BT])
        kv = sb("kv", [128, 2, BT])
        st = sb("st", [128, 2, BT])
        y = sb("y", [128, 2, BT])
        x1t = sb("x1t", [128, 2, BT])
        yt = sb("yt", [128, 2, BT])
        rows = sb("rows", [128, Q, J, ROW])
        lmax = sb("lmax", [128, Q, J])
        ldif = sb("ldif", [128, Q, J, E])
        lexp = sb("lexp", [128, Q, J, E])
        lsum = sb("lsum", [128, Q, J])
        key = sb("key", [128, Q, J, E])
        kmax = sb("kmax", [128, Q, J])
        hot = sb("hot", [128, Q, J, E], BF16)
        cum = sb("cum", [128, Q, E])
        cumb = sb("cumb", [128, Q, E], BF16)
        hsum = sb("hsum", [128, Q, E])
        base = sb("base", [128, Q, J])
        sel = sb("sel", [128, Q, J, E])
        pos = sb("pos", [128, Q, J])
        ofs = sb("ofs", [128, Q, J])
        kept = sb("kept", [128, Q, J])
        slot = sb("slot", [128, Q, J], I32)

        got = sb("got", [128, PAIRS, PC, ROW])
        gt = sb("gt", [128, 2, 2 * CAP])
        hid = sb("hid", [128, 2, FC, CAP])
        ot = sb("ot", [128, 2, 2 * CAP])
        fin = sb("fin", [128, PAIRS, PC, D])

        bank = [ctx.enter_context(nc.psum_tensor(f"bank{i}", [128, 512], F32)) for i in range(8)]
        psT, psK, psV, psR, psO, psX, psY, psS = bank
        logits = psS[:, 0:J * E].rearrange("p (j e) -> p j e", j=J)
        before_ps = psS[:, 64:64 + J * E].rearrange("p (j e) -> p j e", j=J)

        x_in = [sem(f"x_in{q}") for q in range(Q)]
        rot_in, tok_in, par_in, wg_in = sem("rot_in"), sem("tok_in"), sem("par_in"), sem("wg_in")
        wt_in = [sem(f"wt_in{l}") for l in range(NL)]
        wcat_in = [sem(f"wcat_in{b}") for b in range(B)]
        w1_in = [sem(f"w1_in{i}") for i in range(PAIRS)]
        w2_in = [sem(f"w2_in{i}") for i in range(PAIRS)]
        slots_empty = sem("slots_empty")
        zeroed, ident_ok, tri_ok, consts_ok, iotas_ok = (sem("zeroed"), sem("ident_ok"), sem("tri_ok"),
                                                         sem("consts_ok"), sem("iotas_ok"))
        empty_ok, tables_ok, wrow_ok, bias_ok, cat_step = (sem("empty_ok"), sem("tables_ok"), sem("wrow_ok"),
                                                           sem("bias_ok"), sem("cat_step"))
        ang_step, angles_ok, sin_ok, cos_step, amp_ok, rot_ok = (sem("ang_step"), sem("angles_ok"), sem("sin_ok"),
                                                                 sem("cos_step"), sem("amp_ok"), sem("rot_ok"))
        sx_ok, h_ok = sem("sx_ok"), sem("h_ok")
        stat_step, mv_ok, veps_ok, rstd_ok, nrm_ok, tp_ok, xn_ok = (
            sem("stat_step"), sem("mv_ok"), sem("veps_ok"), sem("rstd_ok"), sem("nrm_ok"), sem("tp_ok"), sem("xn_ok"))
        v_mm, r_mm, k_mm, vs_ok, th_ok, kv_ok, st_ok, y_ok, wo_ok, res_ok, xh_ok = (
            sem("v_mm"), sem("r_mm"), sem("k_mm"), sem("vs_ok"), sem("th_ok"), sem("kv_ok"), sem("st_ok"),
            sem("y_ok"), sem("wo_ok"), sem("res_ok"), sem("xh_ok"))
        x1_tp, x1t_ok, lin_ok, yt_ok, yrow_tp, yrow_ok, logit_ok = (
            sem("x1_tp"), sem("x1t_ok"), sem("lin_ok"), sem("yt_ok"), sem("yrow_tp"), sem("yrow_ok"), sem("logit_ok"))
        lmax_ok, ldif_ok, lexp_ok, lsum_ok, gate_ok, key_ok, kmax_ok, hot_ok = (
            sem("lmax_ok"), sem("ldif_ok"), sem("lexp_ok"), sem("lsum_ok"), sem("gate_ok"), sem("key_ok"),
            sem("kmax_ok"), sem("hot_ok"))
        base_ok, hsum_ok, cum_ok, cumb_ok, before_ok, sel_ok, pos_ok, ofs_ok, kept_ok, slot_ok = (
            sem("base_ok"), sem("hsum_ok"), sem("cum_ok"), sem("cumb_ok"), sem("before_ok"), sem("sel_ok"),
            sem("pos_ok"), sem("ofs_ok"), sem("kept_ok"), sem("slot_ok"))
        scattered, out_first = sem("scattered"), sem("out_first")
        in_got = [sem(f"in_got{i}") for i in range(PAIRS)]
        rest_got = [sem(f"rest_got{i}") for i in range(PAIRS)]
        g_tp, gt_a, gt_v, hid_mm, hid_a, hid_v, out_mm, ot_ok, o_tp, fin_ok, out_done = (
            sem("g_tp"), sem("gt_a"), sem("gt_v"), sem("hid_mm"), sem("hid_a"), sem("hid_v"), sem("out_mm"),
            sem("ot_ok"), sem("o_tp"), sem("fin_ok"), sem("out_done"))

        x_q = x.rearrange("(q p) w -> q p w", q=Q)
        out_q = out.rearrange("(q p j) d -> q p j d", q=Q, j=J)
        slots_p = slots[0:SLOTS, :].rearrange("(i c p) w -> i p c w", c=PC, p=128)

        def hid_parts(e):
            return [FC * e + fc for fc in range(FC)]

        block = ctx.enter_context(nc.Block())

        @block.sync
        def _(sp):
            sp.dma_start(rot[:, :], rot_par).then_inc(rot_in, 16)
            sp.dma_start(xt[:, 0, :], x_q[0]).then_inc(x_in[0], 16)
            sp.dma_start(wt[:, 0, :, :], wqkv[:, 0, :, :]).then_inc(wt_in[0], 16)
            sp.dma_start(xt[:, 1, :], x_q[1]).then_inc(x_in[1], 16)
            sp.dma_start(xt[:, 2, :], x_q[2]).then_inc(x_in[2], 16)
            sp.dma_start(xt[:, 3, :], x_q[3]).then_inc(x_in[3], 16)
            sp.dma_start(wt[:, 1, :, :], wqkv[:, 1, :, :]).then_inc(wt_in[1], 16)
            sp.wait_ge(empty_ok, 2)
            for i in range(PAIRS):
                sp.dma_start(slots_p[i], empty[:, :].unsqueeze(1).to_broadcast([128, PC, ROW])
                             ).then_inc(slots_empty, 16)
            for i in range(PAIRS):
                sp.dma_start(w1_sb[:, 2 * i:2 * i + 2, :], w1[:, 2 * i:2 * i + 2, :]).then_inc(w1_in[i], 16)
                sp.dma_start(w2_sb[:, 2 * i:2 * i + 2, :, :], w2[:, 2 * i:2 * i + 2, :, :]).then_inc(w2_in[i], 16)
            for q in range(Q):
                sp.wait_ge(res_ok, Q + q + 1)
                sp.dma_start(out_q[q], rows[:, q, :, D:2 * D]).then_inc(out_first, 16)
            sp.wait_ge(scattered, 16 * Q * J)
            for i in range(PAIRS):
                sp.dma_start(got[:, i, :, 0:D], slots_p[i][:, :, 0:D]).then_inc(in_got[i], 16)
                sp.dma_start(got[:, i, :, D:ROW], slots_p[i][:, :, D:ROW]).then_inc(rest_got[i], 16)

        @block.gpsimd
        def _(pool):
            pool.iota(rowi[:, :], pattern=[[0, 1]], base=0, channel_multiplier=1).then_inc(iotas_ok, 1)
            pool.memset(mhalf[:, :], -0.5).then_inc(consts_ok, 1)
            pool.wait_ge(rot_in, 16)
            pool.tensor_tensor(amp[:, :], rot[:, R_AMP:R_AMP + 1].to_broadcast([128, Q]), rot[:, R_DT:R_DT + Q],
                               ALU.pow).then_inc(amp_ok, 1)
            pool.iota(cati[:, :, :], pattern=[[0, B], [1, NCAT]], base=0, channel_multiplier=0).then_inc(iotas_ok, 1)
            pool.iota(ranki[:, :, :], pattern=[[0, J], [-1, E]], base=E, channel_multiplier=0).then_inc(iotas_ok, 1)
            pool.iota(trashi[:, :, :], pattern=[[BT, Q], [1, J]], base=SLOTS, channel_multiplier=J
                      ).then_inc(iotas_ok, 1)
            pool.memset(identf[:, :], 0.0).then_inc(zeroed, 1)
            pool.wait_ge(zeroed, 1)
            pool.affine_select(out=identf[:, :], in_=identf[:, :], compare_op=ALU.not_equal, fill=1.0, base=0,
                               pattern=[[-1, 128]], channel_multiplier=1).then_inc(ident_ok, 1)
            pool.wait_ge(empty_ok, 1)
            pool.iota(empty[:, TOK:TOK + 1].bitcast(I32), pattern=[[0, 1]], base=NOBODY, channel_multiplier=0
                      ).then_inc(empty_ok, 1)

            def power(n):
                pool.wait_ge(mv_ok, J * (n + 1))
                pool.tensor_scalar(veps[:, n, :], mv[:, n, :, 1], EPS, None, ALU.add).then_inc(veps_ok, 1)
                pool.wait_ge(veps_ok, n + 1)
                if n == 0:
                    pool.wait_ge(consts_ok, 1)
                pool.tensor_tensor(rstd[:, n, :], veps[:, n, :], mhalf[:, :], ALU.pow).then_inc(rstd_ok, 1)

            def gather_maps(b):
                pool.indirect_dma_start(wcat[:, b, :], None, w_cat,
                                        bass.IndirectOffsetOnAxis(ap=wrow[:, b:b + 1], axis=0)
                                        ).then_inc(wcat_in[b], 16)

            def add_x(q):
                pool.wait_ge(res_ok, q + 1)
                pool.tensor_tensor(xh[:, q, :, :], h[:, q, :, :],
                                   xt[:, q, :].rearrange("p (j d) -> p j d", j=J), ALU.add).then_inc(xh_ok, 1)

            power(0)
            for q in range(Q):
                pool.iota(rows[:, q, :, TOK].bitcast(I32), pattern=[[1, J]], base=BT * q, channel_multiplier=J
                          ).then_inc(iotas_ok, 1)
            power(1)
            for t in (before, upto):
                pool.memset(t[:, :], 1.0).then_inc(zeroed, 1)
            pool.memset(onesb[:, :], 1.0).then_inc(consts_ok, 1)
            pool.wait_ge(zeroed, 3)
            pool.affine_select(out=before[:, :], in_=before[:, :], compare_op=ALU.is_gt, fill=0.0, base=0,
                               pattern=[[1, 128]], channel_multiplier=-1).then_inc(tri_ok, 1)
            pool.affine_select(out=upto[:, :], in_=upto[:, :], compare_op=ALU.is_ge, fill=0.0, base=0,
                               pattern=[[1, 128]], channel_multiplier=-1).then_inc(tri_ok, 1)
            power(2)
            pool.wait_ge(wrow_ok, 1)
            for b in range(B):
                gather_maps(b)
                if b == 3:
                    power(3)
            for n in range(Q, NSTEP):
                add_x(n - Q)
                power(n)

            def scatter(q):
                pool.wait_ge(slot_ok, q + 1)
                pool.wait_ge(gate_ok, q + 1)
                pool.wait_ge(yrow_ok, q + 1)
                if q == 0:
                    pool.wait_ge(slots_empty, 16 * PAIRS)
                    pool.wait_ge(iotas_ok, 4 + Q)
                for j in range(J):
                    pool.indirect_dma_start(slots, bass.IndirectOffsetOnAxis(ap=slot[:, q, j:j + 1], axis=0),
                                            rows[:, q, j, :], None).then_inc(scattered, 16)

            for q in range(Q):
                scatter(q)
            pool.wait_ge(out_first, 16 * Q)
            for i in range(PAIRS):
                for c in range(PC):
                    pool.wait_ge(fin_ok, PC * i + c + 1)
                    pool.indirect_dma_start(
                        out, bass.IndirectOffsetOnAxis(ap=got[:, i, c, TOK:TOK + 1].bitcast(I32), axis=0),
                        fin[:, i, c, :], None, bounds_check=NTOK - 1, oob_is_err=False).then_inc(out_done, 16)
            pool.wait_ge(out_done, 16 * PAIRS * PC)

        @block.scalar
        def _(act):
            act.dma_start(tok_id[:, :], itok.to_broadcast([128, B])).then_inc(tok_in, 16)
            act.dma_start(par[:, :], params).then_inc(par_in, 16)
            act.dma_start(wg_sb[:, :], wg).then_inc(wg_in, 16)
            act.wait_ge(angles_ok, 1)
            act.activation(sins[:, :, :], red[:, 2:4, :], ACT.Sin).then_inc(sin_ok, 1)
            act.wait_ge(rot_ok, 1)
            for q in range(Q):
                act.wait_ge(x_in[q], 16)
                act.activation(sx[:, q, :], xt[:, q, :], ACT.Copy, scale=asn[:, q:q + 1]).then_inc(sx_ok, 1)

            def evac_xn(n):
                l = n // Q
                act.wait_ge(tp_ok, n + 1)
                if n == 0:
                    act.wait_ge(par_in, 16)
                if n >= 2:
                    act.wait_ge(r_mm, n - 1)
                act.activation(xn[:, n % 2, :].rearrange("d (p j) -> d j p", j=J),
                               psT[:, :].rearrange("d (j p) -> d j p", j=J), ACT.Identity,
                               bias=par[:, P_LNB + l:P_LNB + l + 1], scale=par[:, P_LNW + l:P_LNW + l + 1]
                               ).then_inc(xn_ok, 1)

            def evac_vr(n):
                act.wait_ge(v_mm, n + 1)
                if n >= 2:
                    act.wait_ge(kv_ok, n - 1)
                act.activation(vs[:, n % 2, :], psV[:, :], ACT.Copy, scale=0.5 * (1.0 - DECAY)).then_inc(vs_ok, 1)
                act.wait_ge(r_mm, n + 1)
                if n >= 2:
                    act.wait_ge(y_ok, n - 1)
                act.activation(th[:, n % 2, :], psR[:, :], ACT.Tanh, scale=0.5).then_inc(th_ok, 1)

            def post_x1t(q):
                act.wait_ge(x1_tp, q + 1)
                if q >= 2:
                    act.wait_ge(lin_ok, q - 1)
                act.activation(x1t[:, q % 2, :], psX[:, :], ACT.Copy).then_inc(x1t_ok, 1)

            def post_yt(q):
                act.wait_ge(lin_ok, q + 1)
                if q == 0:
                    act.wait_ge(bias_ok, 1)
                if q >= 2:
                    act.wait_ge(yrow_tp, q - 1)
                for b2 in range(2):
                    part = [t.rearrange("d (j b f) -> d b j f", j=J, b=2)[:, b2] for t in (yt[:, q % 2, :], psY[:, :])]
                    last = act.activation(part[0], part[1], ACT.Identity, bias=bias[:, 2 * q + b2:2 * q + b2 + 1])
                last.then_inc(yt_ok, 1)

            def post_rows(q):
                act.wait_ge(yrow_tp, q + 1)
                act.activation(rows[:, q, :, 0:D], psX[:, :].rearrange("p (j d) -> p j d", j=J), ACT.Copy
                               ).then_inc(yrow_ok, 1)

            def post_exp(q):
                act.wait_ge(ldif_ok, q + 1)
                act.activation(lexp[:, q, :, :], ldif[:, q, :, :], ACT.Exp).then_inc(lexp_ok, 1)

            for slot_n in range(NSTEP + 3 + 1):
                n = slot_n
                if 1 <= n <= NSTEP:
                    evac_vr(n - 1)
                if n < NSTEP:
                    evac_xn(n)
                q = n - (Q + 2)
                if 0 <= q < Q:
                    post_x1t(q)
                    post_yt(q)
                    post_exp(q)
                    post_rows(q)

            def gather_t(i):
                act.wait_ge(g_tp, i + 1)
                if i >= 2:
                    act.wait_ge(hid_mm, 2 * FC * (i - 1))
                act.activation(gt[:, i % 2, 0:512], bank[0][:, :], ACT.Copy).then_inc(gt_a, 1)

            def relu(e):
                for n in hid_parts(e)[0::2]:
                    act.wait_ge(hid_mm, n + 1)
                    if e >= 2:
                        act.wait_ge(out_mm, e - 1)
                    act.activation(hid[:, e % 2, n % FC, :], bank[2 + n % 3][:, 0:CAP], ACT.Relu,
                                   bias=par[:, P_B1 + n:P_B1 + n + 1]).then_inc(hid_a, 1)

            def out_t(e):
                act.wait_ge(out_mm, e + 1)
                if e >= 4:
                    act.wait_ge(o_tp, e // 2 - 1)
                act.activation(ot[:, (e // 2) % 2, (e % 2) * CAP:(e % 2 + 1) * CAP], bank[5][:, 0:CAP], ACT.Identity,
                               bias=par[:, P_B2 + e:P_B2 + e + 1]).then_inc(ot_ok, 1)

            gather_t(0)
            for e in range(E):
                relu(e)
                if e >= 1:
                    out_t(e - 1)
                if e % 2 and e + 1 < E:
                    gather_t((e + 1) // 2)
            out_t(E - 1)

        @block.tensor
        def _(pe):
            def transposes(n):
                pe.wait_ge(nrm_ok, n + 1)
                if n == 0:
                    pe.wait_ge(ident_ok, 1)
                else:
                    pe.wait_ge(xn_ok, n)
                for j in range(J):
                    last = pe.transpose(psT[:, j * 128:(j + 1) * 128], nrm[:, n % 2, j, :], identf[:, :])
                last.then_inc(tp_ok, 1)

            def project(n):
                l = n // Q
                if n % Q == 0:
                    pe.wait_ge(wt_in[l], 16)
                pe.wait_ge(xn_ok, n + 1)
                if n >= 1:
                    pe.wait_ge(vs_ok, n)
                pe.matmul(psV[:, :], wt[:, l, 1, :], xn[:, n % 2, :], start=True, stop=True).then_inc(v_mm, 1)
                if n >= 1:
                    pe.wait_ge(kv_ok, n)
                pe.matmul(psK[:, :], wt[:, l, 0, :], xn[:, n % 2, :], start=True, stop=True).then_inc(k_mm, 1)
                if n >= 1:
                    pe.wait_ge(th_ok, n)
                pe.matmul(psR[:, :], wt[:, l, 2, :], xn[:, n % 2, :], start=True, stop=True).then_inc(r_mm, 1)

            def mix_out(n):
                l = n // Q
                pe.wait_ge(y_ok, n + 1)
                if n >= 1:
                    pe.wait_ge(res_ok, n)
                yj = y[:, n % 2, :].rearrange("d (p j) -> d j p", j=J)
                for j in range(J):
                    last = pe.matmul(psO[:, j * 128:(j + 1) * 128], yj[:, j, :], wt[:, l, 3, :], start=True, stop=True)
                last.then_inc(wo_ok, 1)

            def post_x1(q):
                pe.wait_ge(res_ok, Q + q + 1)
                if q >= 1:
                    pe.wait_ge(yrow_ok, q)
                for j in range(J):
                    last = pe.transpose(psX[:, j * 128:(j + 1) * 128], rows[:, q, j, D:2 * D], identf[:, :])
                last.then_inc(x1_tp, 1)

            def post_linear(q):
                pe.wait_ge(x1t_ok, q + 1)
                if q >= 1:
                    pe.wait_ge(yt_ok, q)
                for b2 in range(2):
                    pe.wait_ge(wcat_in[2 * q + b2], 16)
                    part = [t.rearrange("d (j b f) -> d b j f", j=J, b=2)[:, b2] for t in (psY[:, :], x1t[:, q % 2, :])]
                    last = pe.matmul(part[0], wcat[:, 2 * q + b2, :], part[1], start=True, stop=True)
                last.then_inc(lin_ok, 1)

            def post_gate(q):
                pe.wait_ge(yt_ok, q + 1)
                if q == 0:
                    pe.wait_ge(wg_in, 16)
                else:
                    pe.wait_ge(ldif_ok, q)
                for j in range(J):
                    last = pe.matmul(logits[:, j, :], yt[:, q % 2, j * 128:(j + 1) * 128], wg_sb[:, :],
                                     start=True, stop=True)
                last.then_inc(logit_ok, 1)
                for j in range(J):
                    last = pe.transpose(psX[:, j * 128:(j + 1) * 128], yt[:, q % 2, j * 128:(j + 1) * 128],
                                        identf[:, :])
                last.then_inc(yrow_tp, 1)

            def post_before(q):
                pe.wait_ge(hot_ok, q + 1)
                if q == 0:
                    pe.wait_ge(tri_ok, 2)
                    pe.wait_ge(consts_ok, 2)
                else:
                    pe.wait_ge(cumb_ok, q)
                    pe.wait_ge(sel_ok, q)
                for j in range(J):
                    terms = [(upto if i < j else before, hot[:, q, i, :]) for i in range(J)]
                    if q:
                        terms.append((onesb, cumb[:, q - 1, :]))
                    for i, (lhsT, rhs) in enumerate(terms):
                        last = pe.matmul(before_ps[:, j, :], lhsT[:, :], rhs, start=(i == 0),
                                         stop=(i == len(terms) - 1))
                last.then_inc(before_ok, 1)

            for n in range(NSTEP + 3 + 1):
                if 0 <= n - 2 < NSTEP:
                    mix_out(n - 2)
                if n < NSTEP:
                    transposes(n)
                    project(n)
                q = n - (Q + 2)
                if 0 <= q < Q:
                    post_x1(q)
                    post_linear(q)
                    post_gate(q)
                    post_before(q)

            def gather_t(i):
                pe.wait_ge(in_got[i], 16)
                if i >= 1:
                    pe.wait_ge(gt_a, i)
                    pe.wait_ge(gt_v, i)
                for c in range(PC):
                    last = pe.transpose(bank[c // 4][:, (c % 4) * 128:(c % 4 + 1) * 128], got[:, i, c, 0:D],
                                        identf[:, :])
                last.then_inc(g_tp, 1)

            def hidden(e):
                i = e // 2
                if e % 2 == 0:
                    pe.wait_ge(w1_in[i], 16)
                    pe.wait_ge(gt_a, i + 1)
                    pe.wait_ge(gt_v, i + 1)
                for n in hid_parts(e):
                    if n >= 3:
                        pe.wait_ge(hid_v if (n - 3) % 2 else hid_a, (n - 3) // 2 + 1)
                    pe.matmul(bank[2 + n % 3][:, 0:CAP], w1_sb[:, e, (n % FC) * 128:(n % FC + 1) * 128],
                              gt[:, i % 2, (e % 2) * CAP:(e % 2 + 1) * CAP], start=True, stop=True
                              ).then_inc(hid_mm, 1)

            def outer(e):
                if e % 2 == 0:
                    pe.wait_ge(w2_in[e // 2], 16)
                if e >= 1:
                    pe.wait_ge(ot_ok, e)
                for n in hid_parts(e):
                    pe.wait_ge(hid_v if n % 2 else hid_a, n // 2 + 1)
                    last = pe.matmul(bank[5][:, 0:CAP], w2_sb[:, e, n % FC, :], hid[:, e % 2, n % FC, :],
                                     start=(n % FC == 0), stop=(n % FC == FC - 1))
                last.then_inc(out_mm, 1)

            def back(i):
                pe.wait_ge(ot_ok, 2 * i + 2)
                if i >= 1:
                    pe.wait_ge(fin_ok, PC * i)
                for c in range(PC):
                    last = pe.transpose(bank[6 + c // 4][:, (c % 4) * 128:(c % 4 + 1) * 128],
                                        ot[:, i % 2, c * 128:(c + 1) * 128], identf[:, :])
                last.then_inc(o_tp, 1)

            gather_t(0)
            hidden(0)
            for e in range(E):
                if e + 1 < E:
                    if e % 2:
                        gather_t((e + 1) // 2)
                    hidden(e + 1)
                outer(e)
                if e % 2 == 0 and e:
                    back(e // 2 - 1)
            back(PAIRS - 1)

        @block.vector
        def _(dve):
            steps = {}

            def link(ins, s):
                steps[s.name] = steps.get(s.name, 0) + 1
                ins.then_inc(s, 1)
                dve.wait_ge(s, steps[s.name])

            dve.wait_ge(rot_in, 16)
            link(dve.tensor_scalar(ang[:, :], rot[:, R_DT:R_DT + Q], rot[:, R_FREQ:R_FREQ + 1], None, ALU.mult),
                 ang_step)
            link(dve.tensor_scalar(turns[:, 0, :], ang[:, :], 1.0 / TWO_PI, ROUND, ALU.mult, ALU.add), ang_step)
            link(dve.tensor_scalar(turns[:, 1, :], turns[:, 0, :], -ROUND, None, ALU.add), ang_step)
            link(dve.scalar_tensor_tensor(red[:, 0, :], turns[:, 1, :], -C1, ang[:, :], ALU.mult, ALU.add), ang_step)
            link(dve.scalar_tensor_tensor(red[:, 1, :], turns[:, 1, :], -C2, red[:, 0, :], ALU.mult, ALU.add),
                 ang_step)
            link(dve.scalar_tensor_tensor(red[:, 0, :], turns[:, 1, :], -C3, red[:, 1, :], ALU.mult, ALU.add),
                 ang_step)
            dve.tensor_scalar(red[:, 2, :], red[:, 0, :], 0.5, None, ALU.mult)
            dve.tensor_scalar(red[:, 3, :], red[:, 0, :], PI_IN, -PI_IN, ALU.min, ALU.max).then_inc(angles_ok, 1)
            dve.memset(empty[:, :], 0.0).then_inc(empty_ok, 1)
            dve.wait_ge(sin_ok, 1)
            link(dve.tensor_tensor(cosr[:, 0, :], sins[:, 0, :], sins[:, 0, :], ALU.mult), cos_step)
            link(dve.tensor_scalar(cosr[:, 1, :], cosr[:, 0, :], -2.0, 1.0, ALU.mult, ALU.add), cos_step)
            dve.wait_ge(amp_ok, 1)
            dve.tensor_tensor(asn[:, :], amp[:, :], sins[:, 1, :], ALU.mult).then_inc(rot_ok, 1)
            link(dve.tensor_tensor(ac[:, :], amp[:, :], cosr[:, 1, :], ALU.mult), cos_step)

            def rotate(q):
                half = BT // 2
                hq = h[:, q, :, :].rearrange("p j d -> p (j d)")
                dve.wait_ge(sx_ok, q + 1)
                dve.scalar_tensor_tensor(hq[:, 0:half], xt[:, q, 0:half], ac[:, q:q + 1], sx[:, q, half:BT],
                                         ALU.mult, ALU.subtract)
                dve.scalar_tensor_tensor(hq[:, half:BT], xt[:, q, half:BT], ac[:, q:q + 1], sx[:, q, 0:half],
                                         ALU.mult, ALU.add).then_inc(h_ok, 1)

            def norm_stats(n):
                q = n % Q
                if n < Q:
                    dve.wait_ge(h_ok, q + 1)
                else:
                    dve.wait_ge(res_ok, q + 1)
                for j in range(J):
                    dve.bn_stats(stats[:, n, j, :], h[:, q, j, :]).then_inc(stat_step, 1)
                for j in range(J):
                    dve.wait_ge(stat_step, J * n + j + 1)
                    dve.bn_aggr(mv[:, n, j, :], stats[:, n, j, :]).then_inc(mv_ok, 1)

            def normalize(n):
                dve.wait_ge(rstd_ok, n + 1)
                if n >= 2:
                    dve.wait_ge(tp_ok, n - 1)
                for j in range(J):
                    last = dve.tensor_scalar(nrm[:, n % 2, j, :], h[:, n % Q, j, :], mv[:, n, j, 0:1],
                                             rstd[:, n, j:j + 1], ALU.subtract, ALU.mult)
                last.then_inc(nrm_ok, 1)

            def times(n):
                dve.wait_ge(k_mm, n + 1)
                dve.wait_ge(vs_ok, n + 1)
                dve.tensor_tensor(kv[:, n % 2, :], psK[:, :], vs[:, n % 2, :], ALU.mult).then_inc(kv_ok, 1)

            def scan(n):
                dve.wait_ge(kv_ok, n + 1)
                if n == 0:
                    dve.wait_ge(tables_ok, 2)
                dve.tensor_tensor_scan(st[:, n % 2, :], decay[:, :], kv[:, n % 2, :], 0.0, ALU.mult, ALU.add
                                       ).then_inc(st_ok, 1)

            def gate_y(n):
                dve.wait_ge(st_ok, n + 1)
                dve.wait_ge(th_ok, n + 1)
                if n >= 2:
                    dve.wait_ge(wo_ok, n - 1)
                dve.scalar_tensor_tensor(y[:, n % 2, :], th[:, n % 2, :], 1.0, st[:, n % 2, :], ALU.add, ALU.mult
                                         ).then_inc(y_ok, 1)

            def residual(n):
                q = n % Q
                dve.wait_ge(wo_ok, n + 1)
                ps = psO[:, :].rearrange("p (j d) -> p j d", j=J)
                if n < Q:
                    dve.tensor_tensor(h[:, q, :, :], ps, h[:, q, :, :], ALU.add).then_inc(res_ok, 1)
                else:
                    dve.wait_ge(xh_ok, q + 1)
                    dve.tensor_tensor(rows[:, q, :, D:2 * D], ps, xh[:, q, :, :], ALU.add).then_inc(res_ok, 1)

            def tables():
                dve.memset(decay[:, :], DECAY).then_inc(tables_ok, 1)
                dve.wait_ge(tables_ok, 1)
                dve.memset(decay[:, :].rearrange("p (b t) -> p b t", b=2)[:, :, 0:1], 0.0).then_inc(tables_ok, 1)

            def category():
                dve.wait_ge(iotas_ok, 4)
                dve.wait_ge(tok_in, 16)
                dve.tensor_copy(rowf[:, :], rowi[:, :])
                dve.tensor_copy(catf[:, :, :], cati[:, :, :])
                dve.tensor_copy(rank[:, :, :], ranki[:, :, :])
                dve.tensor_copy(trash[:, :, :], trashi[:, :, :])
                link(dve.tensor_copy(idf[:, :], tok_id[:, :]), cat_step)
                dve.tensor_scalar(wrow[:, :], idf[:, :], float(D), rowf[:, 0:1], ALU.mult, ALU.add
                                  ).then_inc(wrow_ok, 1)
                link(dve.tensor_tensor(cat_hot[:, :, :], catf[:, :, :],
                                       idf[:, :].unsqueeze(2).to_broadcast([128, B, NCAT]), ALU.is_equal), cat_step)
                dve.wait_ge(par_in, 16)
                link(dve.tensor_tensor(cat_sel[:, :, :], cat_hot[:, :, :],
                                       par[:, P_BIAS:P_BIAS + NCAT].unsqueeze(1).to_broadcast([128, B, NCAT]),
                                       ALU.mult), cat_step)
                dve.tensor_reduce(bias[:, :], cat_sel[:, :, :], AX_X, ALU.add).then_inc(bias_ok, 1)

            def gate(q):
                dve.wait_ge(logit_ok, q + 1)
                link(dve.tensor_reduce(lmax[:, q, :], logits, AX_X, ALU.max), lmax_ok)
                dve.tensor_tensor(ldif[:, q, :, :], logits, lmax[:, q, :].unsqueeze(2).to_broadcast([128, J, E]),
                                  ALU.subtract).then_inc(ldif_ok, 1)
                dve.wait_ge(ldif_ok, q + 1)
                link(dve.scalar_tensor_tensor(key[:, q, :, :], ldif[:, q, :, :], 0.0, rank[:, :, :],
                                              ALU.is_ge, ALU.mult), key_ok)
                link(dve.tensor_reduce(kmax[:, q, :], key[:, q, :, :], AX_X, ALU.max), kmax_ok)
                dve.tensor_tensor(hot[:, q, :, :], key[:, q, :, :],
                                  kmax[:, q, :].unsqueeze(2).to_broadcast([128, J, E]), ALU.is_equal
                                  ).then_inc(hot_ok, 1)
                dve.scalar_tensor_tensor(base[:, q, :], kmax[:, q, :], -float(CAP), trash[:, q, :],
                                         ALU.mult, ALU.subtract).then_inc(base_ok, 1)
                dve.wait_ge(hot_ok, q + 1)
                if q + 1 < Q:
                    link(dve.tensor_reduce(hsum[:, q, :], hot[:, q, :, :].rearrange("p j e -> p e j"), AX_X, ALU.add),
                         hsum_ok)
                    if q:
                        dve.tensor_tensor(cum[:, q, :], cum[:, q - 1, :], hsum[:, q, :], ALU.add).then_inc(cum_ok, 1)
                    else:
                        dve.tensor_copy(cum[:, q, :], hsum[:, q, :]).then_inc(cum_ok, 1)
                    dve.wait_ge(cum_ok, q + 1)
                    dve.tensor_copy(cumb[:, q, :], cum[:, q, :]).then_inc(cumb_ok, 1)
                dve.wait_ge(lexp_ok, q + 1)
                link(dve.tensor_reduce(lsum[:, q, :], lexp[:, q, :, :], AX_X, ALU.add), lsum_ok)
                dve.reciprocal(rows[:, q, :, GATE], lsum[:, q, :]).then_inc(gate_ok, 1)

            def place(q):
                dve.wait_ge(before_ok, q + 1)
                link(dve.tensor_tensor(sel[:, q, :, :], before_ps, hot[:, q, :, :], ALU.mult), sel_ok)
                link(dve.tensor_reduce(pos[:, q, :], sel[:, q, :, :], AX_X, ALU.add), pos_ok)
                dve.wait_ge(base_ok, q + 1)
                link(dve.scalar_tensor_tensor(ofs[:, q, :], pos[:, q, :], float(SLOTS), base[:, q, :],
                                              ALU.add, ALU.add), ofs_ok)
                link(dve.scalar_tensor_tensor(kept[:, q, :], pos[:, q, :], float(CAP), ofs[:, q, :],
                                              ALU.is_lt, ALU.mult), kept_ok)
                dve.tensor_tensor(slot[:, q, :], kept[:, q, :], trash[:, q, :], ALU.add).then_inc(slot_ok, 1)

            for n in range(NSTEP + 3 + 1):
                if n < Q:
                    rotate(n)
                if n < NSTEP:
                    norm_stats(n)
                if n == 0:
                    tables()
                if 0 <= n - 1 < NSTEP:
                    times(n - 1)
                if n < NSTEP:
                    normalize(n)
                if n == 0:
                    category()
                if 0 <= n - 1 < NSTEP:
                    scan(n - 1)
                if 0 <= n - 2 < NSTEP:
                    residual(n - 2)
                if 0 <= n - 1 < NSTEP:
                    gate_y(n - 1)
                q = n - (Q + 2)
                if 0 <= q < Q:
                    gate(q)
                    place(q)

            def gather_t(i):
                dve.wait_ge(g_tp, i + 1)
                if i >= 2:
                    dve.wait_ge(hid_mm, 2 * FC * (i - 1))
                dve.tensor_copy(gt[:, i % 2, 512:2 * CAP], bank[1][:, 0:2 * CAP - 512]).then_inc(gt_v, 1)

            def relu(e):
                for n in hid_parts(e)[1::2]:
                    dve.wait_ge(hid_mm, n + 1)
                    if e >= 2:
                        dve.wait_ge(out_mm, e - 1)
                    dve.tensor_scalar(hid[:, e % 2, n % FC, :], bank[2 + n % 3][:, 0:CAP],
                                      par[:, P_B1 + n:P_B1 + n + 1], 0.0, ALU.add, ALU.max).then_inc(hid_v, 1)

            def finish(i):
                dve.wait_ge(o_tp, i + 1)
                dve.wait_ge(rest_got[i], 16)
                for c in range(PC):
                    dve.scalar_tensor_tensor(fin[:, i, c, :], bank[6 + c // 4][:, (c % 4) * 128:(c % 4 + 1) * 128],
                                             got[:, i, c, GATE:GATE + 1], got[:, i, c, D:2 * D], ALU.mult, ALU.add
                                             ).then_inc(fin_ok, 1)

            gather_t(0)
            for e in range(E):
                relu(e)
                if e % 2 and e + 1 < E:
                    gather_t((e + 1) // 2)
                if e % 2 and e > 1:
                    finish(e // 2 - 1)
            finish(PAIRS - 1)


def kernel(**inputs):
    import numpy as np
    import concourse.bacc as bacc
    from concourse.bass_utils import run_bass_kernel_spmd

    a = {k: np.asarray(v) for k, v in inputs.items()}

    def cols(v):
        return v.reshape(-1, D).T

    laid = {
        "x": a["x"].reshape(Q * 128, BT),
        "rot_par": np.concatenate([
            np.repeat(a["condB_deltat"].reshape(Q, 2).T, S // J, axis=0),
            np.tile(a["L0_cond_amplitudes"], 2)[:, None],
            np.tile(a["L0_cond_frequencies"], 2)[:, None]], axis=1),
        "itok": a["itok_B_0_15"].reshape(1, B),
        "params": np.concatenate([cols(a["L0_attn_ln_w"]), cols(a["L0_attn_ln_b"]), cols(a["L0_ffn_b1"]),
                                  cols(a["L0_ffn_b2"]), cols(a["L0_cond2_bias"])], axis=1),
        "wqkv": np.stack([a["L0_attn_Wk"], a["L0_attn_Wv"], a["L0_attn_Wr"], a["L0_attn_Wo"]],
                         axis=1).transpose(3, 0, 1, 2),
        "w_cat": a["L0_cond2_weight"].reshape(NCAT * D, D),
        "wg": a["L0_ffn_wg"],
        "w1": a["L0_ffn_w1"].transpose(1, 0, 2),
        "w2": a["L0_ffn_w2"].reshape(E, FC, D, D).transpose(2, 0, 1, 3),
    }
    nc = bacc.Bacc("TRN2", target_bir_lowering=False, num_devices=1)
    arrays, args = {}, []
    for name, v in laid.items():
        v = np.ascontiguousarray(v)
        arrays[name] = v
        args.append(nc.dram_tensor(name, v.shape, mybir.dt.from_np(v.dtype), kind="ExternalInput").ap())
    out = nc.dram_tensor("out", (NTOK, D), F32, kind="ExternalOutput").ap()
    build(nc, *args, out)
    r = run_bass_kernel_spmd(nc, [arrays], core_ids=[0])
    return r.results[0]["out"].reshape(B, S, D)
```

```python
from contextlib import ExitStack

import concourse.bass as bass
from concourse import mybir

ALU = mybir.AluOpType
ACT = mybir.ActivationFunctionType
AX_X = mybir.AxisListType.X
F32 = mybir.dt.float32
BF16 = mybir.dt.bfloat16
I32 = mybir.dt.int32

B, S, D = 8, 256, 128
J = 4
Q = 4
BT = B * S // Q
NL = 2
E, DFF = 8, 512
FC = DFF // D
NCAT = 16
NTOK = B * S
CAP = int(1.25 * NTOK / E)
SLOTS = E * CAP
PAIRS = E // 2
PC = 2 * CAP // 128
CHUNKS = [range(CAP // 128), range(CAP // 128, PC)]
REM = 128 - CAP % 128
LAST_ORDER = [0, 1, 3, 2, 4]
ROW = 2 * D + 2
GATE, TOK = 2 * D, 2 * D + 1
NOBODY = 1 << 20
DECAY = 0.95
EPS = 1e-5
WARM = 57
HALF = 2
NSTEP = Q * NL
TURNS = Q + 9

P_LNW, P_LNB, P_B1, P_B2, P_BIAS = 0, NL, 2 * NL, 2 * NL + E * FC, 2 * NL + E * FC + E
NPAR = P_BIAS + NCAT
R_DT, R_AMP, R_FREQ = 0, Q, Q + 1
NROT = Q + 2

TWO_PI = 6.283185307179586
C1 = 6.28125
C2 = TWO_PI - C1
PI_IN = 3.1415925
ROUND = 12582912.0


def build(nc, x, rot_par, itok, params, wqkv, w_cat, wg, w1, w2, b2_last, out):
    ctx = ExitStack()
    with ctx:
        def sb(name, shape, dt=F32):
            return ctx.enter_context(nc.sbuf_tensor(name, shape, dt))

        def sem(name):
            return ctx.enter_context(nc.semaphore(name))

        slots = nc.dram_tensor("slots", (SLOTS + NTOK, ROW), F32).ap()

        xt = sb("xt", [128, Q, BT])
        rot = sb("rot", [128, NROT])
        par = sb("par", [128, NPAR])
        tok_id = sb("tok_id", [128, B], I32)
        wt = sb("wt", [128, NL, 4, D])
        wcat = sb("wcat", [128, B, D])
        wg_sb = sb("wg_sb", [128, E])
        w1_sb = sb("w1_sb", [128, E, DFF])
        w2_sb = sb("w2_sb", [128, E, FC, D])

        b2row = sb("b2row", [128, D])

        identf = sb("identf", [128, 128])
        before = sb("before", [128, 128], BF16)
        identb = sb("identb", [128, 128], BF16)
        onesb = sb("onesb", [128, 128], BF16)
        decay = sb("decay", [128, BT])
        empty = sb("empty", [128, ROW])
        warm = sb("warm", [128, 512], BF16)
        mhalf = sb("mhalf", [128, J])
        rank = sb("rank", [128, J, E])
        ranki = sb("ranki", [128, J, E], I32)
        trashi = sb("trashi", [128, Q, J], I32)
        trash = sb("trash", [128, Q, J])
        cati = sb("cati", [128, B, NCAT], I32)
        catf = sb("catf", [128, B, NCAT])
        rowi = sb("rowi", [128, 1], I32)
        rowf = sb("rowf", [128, 1])
        idf = sb("idf", [128, B])
        wrow = sb("wrow", [128, B], I32)
        cat_hot = sb("cat_hot", [128, B, NCAT])
        cat_sel = sb("cat_sel", [128, B, NCAT])
        bias = sb("bias", [128, B])

        ang = sb("ang", [128, Q])
        turns = sb("turns", [128, 2, Q])
        red = sb("red", [128, 4, Q])
        sins = sb("sins", [128, 2, Q])
        cosr = sb("cosr", [128, 2, Q])
        amp = sb("amp", [128, Q])
        ac = sb("ac", [128, Q])
        asn = sb("asn", [128, Q])
        sx = sb("sx", [128, Q, BT])
        h = sb("h", [128, Q, J, D])
        xh = sb("xh", [128, Q, J, D])
        stats = sb("stats", [128, NSTEP, J, 6])
        mv = sb("mv", [128, NSTEP, J, 2])
        veps = sb("veps", [128, NSTEP, J])
        rstd = sb("rstd", [128, NSTEP, J])
        nmean = sb("nmean", [128, NSTEP, J - HALF])
        shift = sb("shift", [128, NSTEP, J - HALF])
        nrm = sb("nrm", [128, 2, J, D])
        xn = sb("xn", [128, 2, BT])
        vs = sb("vs", [128, 2, BT])
        th = sb("th", [128, 2, BT])
        kv = sb("kv", [128, 2, BT])
        st = sb("st", [128, 2, BT])
        y = sb("y", [128, 2, BT])
        x1t = sb("x1t", [128, 2, BT])
        yt = sb("yt", [128, 2, BT])
        rows = sb("rows", [128, Q, J, ROW])
        lmax = sb("lmax", [128, Q, J])
        ldif = sb("ldif", [128, Q, J, E])
        lexp = sb("lexp", [128, Q, J, E])
        lsum = sb("lsum", [128, Q, J])
        key = sb("key", [128, Q, J, E])
        kmax = sb("kmax", [128, Q, J])
        hot = sb("hot", [128, Q, J, E], BF16)
        base = sb("base", [128, Q, J])
        sel = sb("sel", [128, Q, J, E])
        pos = sb("pos", [128, Q, J])
        ofs = sb("ofs", [128, Q, J])
        kept = sb("kept", [128, Q, J])
        slot = sb("slot", [128, Q, J], I32)

        got = sb("got", [128, PAIRS, PC, ROW])
        gt = sb("gt", [128, 2, 2 * CAP])
        hid = sb("hid", [128, 2, FC, CAP])
        ot = sb("ot", [128, 2, 2 * CAP])
        res_b2 = sb("res_b2", [128, 2, D])
        fin = sb("fin", [128, PAIRS, PC, D])

        bank = [ctx.enter_context(nc.psum_tensor(f"bank{i}", [128, 512], F32)) for i in range(8)]
        psT, psK, psV, psR, psO, psX, psY, psS = bank
        logits = psS[:, 0:J * E].rearrange("p (j e) -> p j e", j=J)
        before_ps = psV[:, 0:J * E].rearrange("p (j e) -> p j e", j=J)

        x_in = [sem(f"x_in{q}") for q in range(Q)]
        rot_in, tok_in, par_in, wg_in = sem("rot_in"), sem("tok_in"), sem("par_in"), sem("wg_in")
        wt_in = [sem(f"wt_in{l}") for l in range(NL)]
        wcat_in = [sem(f"wcat_in{b}") for b in range(B)]
        w1_in = [sem(f"w1_in{i}") for i in range(PAIRS)]
        w2_in = [sem(f"w2_in{i}") for i in range(PAIRS)]
        slots_empty = sem("slots_empty")
        zeroed, ident_ok, tri_ok, consts_ok, iotas_ok = (sem("zeroed"), sem("ident_ok"), sem("tri_ok"),
                                                         sem("consts_ok"), sem("iotas_ok"))
        empty_ok, tables_ok, wrow_ok, bias_ok, cat_step = (sem("empty_ok"), sem("tables_ok"), sem("wrow_ok"),
                                                           sem("bias_ok"), sem("cat_step"))
        ang_step, angles_ok, sin_ok, cos_step, amp_ok, rot_ok = (sem("ang_step"), sem("angles_ok"), sem("sin_ok"),
                                                                 sem("cos_step"), sem("amp_ok"), sem("rot_ok"))
        sx_ok, h_ok = sem("sx_ok"), sem("h_ok")
        nmean_ok, shift_ok, nrm_a, nrm_v = sem("nmean_ok"), sem("shift_ok"), sem("nrm_a"), sem("nrm_v")
        stat_step, mv_ok, veps_ok, rstd_ok, tp_ok, xn_ok = (
            sem("stat_step"), sem("mv_ok"), sem("veps_ok"), sem("rstd_ok"), sem("tp_ok"), sem("xn_ok"))
        v_mm, r_mm, k_mm, vs_ok, th_ok, kv_ok, st_ok, y_ok, wo_ok, res_ok, xh_ok = (
            sem("v_mm"), sem("r_mm"), sem("k_mm"), sem("vs_ok"), sem("th_ok"), sem("kv_ok"), sem("st_ok"),
            sem("y_ok"), sem("wo_ok"), sem("res_ok"), sem("xh_ok"))
        x1_tp, x1t_ok, lin_ok, yt_ok, yrow_tp, yrow_ok, logit_ok = (
            sem("x1_tp"), sem("x1t_ok"), sem("lin_ok"), sem("yt_ok"), sem("yrow_tp"), sem("yrow_ok"), sem("logit_ok"))
        lmax_ok, ldif_ok, lexp_ok, lsum_ok, gate_ok, key_ok, kmax_ok, hot_ok = (
            sem("lmax_ok"), sem("ldif_ok"), sem("lexp_ok"), sem("lsum_ok"), sem("gate_ok"), sem("key_ok"),
            sem("kmax_ok"), sem("hot_ok"))
        base_ok, before_ok, sel_ok, pos_ok, ofs_ok, kept_ok, slot_ok = (
            sem("base_ok"), sem("before_ok"), sem("sel_ok"),
            sem("pos_ok"), sem("ofs_ok"), sem("kept_ok"), sem("slot_ok"))
        scattered, out_first = sem("scattered"), sem("out_first")
        in_got = [sem(f"in_got{i}") for i in range(PAIRS)]
        b2_in, direct_mm, res_b2_ok = sem("b2_in"), sem("direct_mm"), sem("res_b2_ok")
        rest_got = [sem(f"rest_got{i}") for i in range(PAIRS)]
        g_tp, gt_a, gt_v, hid_mm, hid_a, hid_v, out_mm, ot_ok, o_tp, fin_ok, out_done = (
            sem("g_tp"), sem("gt_a"), sem("gt_v"), sem("hid_mm"), sem("hid_a"), sem("hid_v"), sem("out_mm"),
            sem("ot_ok"), sem("o_tp"), sem("fin_ok"), sem("out_done"))

        x_q = x.rearrange("(q p) w -> q p w", q=Q)
        out_q = out.rearrange("(q p j) d -> q p j d", q=Q, j=J)
        slots_p = slots[0:SLOTS, :].rearrange("(i c p) w -> i p c w", c=PC, p=128)

        def hid_parts(e):
            return [FC * e + fc for fc in range(FC)]

        block = ctx.enter_context(nc.Block())

        @block.sync
        def _(sp):
            sp.dma_start(rot[:, :], rot_par).then_inc(rot_in, 16)
            sp.dma_start(xt[:, 0, :], x_q[0]).then_inc(x_in[0], 16)
            sp.dma_start(xt[:, 1, :], x_q[1]).then_inc(x_in[1], 16)
            sp.dma_start(par[:, :], params).then_inc(par_in, 16)
            sp.dma_start(wt[:, 0, :, :], wqkv[:, 0, :, :]).then_inc(wt_in[0], 16)
            sp.dma_start(tok_id[:, :], itok.to_broadcast([128, B])).then_inc(tok_in, 16)
            sp.dma_start(xt[:, 2, :], x_q[2]).then_inc(x_in[2], 16)
            sp.dma_start(xt[:, 3, :], x_q[3]).then_inc(x_in[3], 16)
            sp.dma_start(wt[:, 1, :, :], wqkv[:, 1, :, :]).then_inc(wt_in[1], 16)
            sp.dma_start(wg_sb[:, :], wg).then_inc(wg_in, 16)
            sp.wait_ge(empty_ok, 2)
            for i in range(PAIRS):
                sp.dma_start(slots_p[i], empty[:, :].unsqueeze(1).to_broadcast([128, PC, ROW])
                             ).then_inc(slots_empty, 16)
            for i in range(PAIRS):
                sp.dma_start(w1_sb[:, 2 * i:2 * i + 2, :], w1[:, 2 * i:2 * i + 2, :]).then_inc(w1_in[i], 16)
                sp.dma_start(w2_sb[:, 2 * i:2 * i + 2, :, :], w2[:, 2 * i:2 * i + 2, :, :]).then_inc(w2_in[i], 16)
            sp.dma_start(b2row[:, :], b2_last.to_broadcast([128, D])).then_inc(b2_in, 16)
            for q in range(Q):
                sp.wait_ge(res_ok, Q + q + 1)
                sp.dma_start(out_q[q], rows[:, q, :, D:2 * D]).then_inc(out_first, 16)
            sp.wait_ge(scattered, 16 * Q * J)
            for i in range(PAIRS):
                sp.dma_start(got[:, i, :, 0:D], slots_p[i][:, :, 0:D]).then_inc(in_got[i], 16)
                sp.dma_start(got[:, i, :, D:ROW], slots_p[i][:, :, D:ROW]).then_inc(rest_got[i], 16)

        @block.gpsimd
        def _(pool):
            pool.iota(rowi[:, :], pattern=[[0, 1]], base=0, channel_multiplier=1).then_inc(iotas_ok, 1)
            pool.memset(mhalf[:, :], -0.5).then_inc(consts_ok, 1)
            pool.wait_ge(rot_in, 16)
            pool.tensor_tensor(amp[:, :], rot[:, R_AMP:R_AMP + 1].to_broadcast([128, Q]), rot[:, R_DT:R_DT + Q],
                               ALU.pow).then_inc(amp_ok, 1)
            pool.iota(cati[:, :, :], pattern=[[0, B], [1, NCAT]], base=0, channel_multiplier=0).then_inc(iotas_ok, 1)
            pool.iota(ranki[:, :, :], pattern=[[0, J], [-1, E]], base=E, channel_multiplier=0).then_inc(iotas_ok, 1)
            pool.iota(trashi[:, :, :], pattern=[[BT, Q], [1, J]], base=SLOTS, channel_multiplier=J
                      ).then_inc(iotas_ok, 1)
            pool.memset(identf[:, :], 0.0).then_inc(zeroed, 1)
            pool.wait_ge(zeroed, 1)
            pool.affine_select(out=identf[:, :], in_=identf[:, :], compare_op=ALU.not_equal, fill=1.0, base=0,
                               pattern=[[-1, 128]], channel_multiplier=1).then_inc(ident_ok, 1)
            pool.wait_ge(empty_ok, 1)
            pool.iota(empty[:, TOK:TOK + 1].bitcast(I32), pattern=[[0, 1]], base=NOBODY, channel_multiplier=0
                      ).then_inc(empty_ok, 1)

            def power(n):
                pool.wait_ge(mv_ok, J * (n + 1))
                pool.tensor_scalar(veps[:, n, :], mv[:, n, :, 1], EPS, None, ALU.add).then_inc(veps_ok, 1)
                pool.tensor_scalar(nmean[:, n, :], mv[:, n, HALF:J, 0], -1.0, None, ALU.mult).then_inc(nmean_ok, 1)
                pool.wait_ge(veps_ok, n + 1)
                if n == 0:
                    pool.wait_ge(consts_ok, 1)
                pool.tensor_tensor(rstd[:, n, :], veps[:, n, :], mhalf[:, :], ALU.pow).then_inc(rstd_ok, 1)
                pool.wait_ge(rstd_ok, n + 1)
                pool.wait_ge(nmean_ok, n + 1)
                pool.tensor_tensor(shift[:, n, :], nmean[:, n, :], rstd[:, n, HALF:J], ALU.mult).then_inc(shift_ok, 1)

            def gather_maps(b):
                pool.indirect_dma_start(wcat[:, b, :], None, w_cat,
                                        bass.IndirectOffsetOnAxis(ap=wrow[:, b:b + 1], axis=0)
                                        ).then_inc(wcat_in[b], 16)

            def add_x(q):
                pool.wait_ge(res_ok, q + 1)
                pool.tensor_tensor(xh[:, q, :, :], h[:, q, :, :],
                                   xt[:, q, :].rearrange("p (j d) -> p j d", j=J), ALU.add).then_inc(xh_ok, 1)

            power(0)
            pool.wait_ge(ident_ok, 1)
            for q in range(Q):
                pool.iota(rows[:, q, :, TOK].bitcast(I32), pattern=[[1, J]], base=BT * q, channel_multiplier=J
                          ).then_inc(iotas_ok, 1)
            power(1)
            pool.memset(before[:, :], 1.0).then_inc(zeroed, 1)
            pool.tensor_copy(identb[:, :], identf[:, :]).then_inc(consts_ok, 1)
            pool.memset(onesb[:, :], 1.0).then_inc(consts_ok, 1)
            pool.memset(warm[:, :], 1.0).then_inc(consts_ok, 1)
            pool.wait_ge(zeroed, 2)
            pool.affine_select(out=before[:, :], in_=before[:, :], compare_op=ALU.is_gt, fill=0.0, base=0,
                               pattern=[[1, 128]], channel_multiplier=-1).then_inc(tri_ok, 1)
            power(2)
            power(3)
            pool.wait_ge(wrow_ok, 1)
            for n in range(Q, NSTEP):
                power(n)
                add_x(n - Q)
                gather_maps(2 * (n - Q))
                gather_maps(2 * (n - Q) + 1)

            def scatter(q):
                pool.wait_ge(slot_ok, q + 1)
                pool.wait_ge(gate_ok, q + 1)
                pool.wait_ge(yrow_ok, q + 1)
                if q == 0:
                    pool.wait_ge(slots_empty, 16 * PAIRS)
                    pool.wait_ge(iotas_ok, 4 + Q)
                for j in range(J):
                    pool.indirect_dma_start(slots, bass.IndirectOffsetOnAxis(ap=slot[:, q, j:j + 1], axis=0),
                                            rows[:, q, j, :], None).then_inc(scattered, 16)

            for q in range(Q):
                scatter(q)
            pool.wait_ge(out_first, 16 * Q)
            for i in range(PAIRS):
                for n, c in enumerate(LAST_ORDER if i == PAIRS - 1 else range(PC)):
                    pool.wait_ge(fin_ok, PC * i + n + 1)
                    pool.indirect_dma_start(
                        out, bass.IndirectOffsetOnAxis(ap=got[:, i, c, TOK:TOK + 1].bitcast(I32), axis=0),
                        fin[:, i, c, :], None, bounds_check=NTOK - 1, oob_is_err=False).then_inc(out_done, 16)
            pool.wait_ge(out_done, 16 * PAIRS * PC)

        @block.scalar
        def _(act):
            act.preload_act_table(ACT.Sin)
            act.wait_ge(angles_ok, 1)
            act.activation(sins[:, :, :], red[:, 2:4, :], ACT.Sin).then_inc(sin_ok, 1)
            act.wait_ge(rot_ok, 1)
            for q in range(Q):
                act.wait_ge(x_in[q], 16)
                act.activation(sx[:, q, :], xt[:, q, :], ACT.Copy, scale=asn[:, q:q + 1]).then_inc(sx_ok, 1)
            act.preload_act_table(ACT.Exp)

            def normalize(n):
                act.wait_ge(shift_ok, n + 1)
                act.wait_ge(rstd_ok, n + 1)
                if n < Q:
                    act.wait_ge(h_ok, n + 1)
                else:
                    act.wait_ge(res_ok, n - Q + 1)
                if n >= 2:
                    act.wait_ge(tp_ok, n - 1)
                for j in range(HALF, J):
                    last = act.activation(nrm[:, n % 2, j, :], h[:, n % Q, j, :], ACT.Identity,
                                          bias=shift[:, n, j - HALF:j - HALF + 1], scale=rstd[:, n, j:j + 1])
                last.then_inc(nrm_a, 1)

            def evac_xn(n):
                l = n // Q
                act.wait_ge(tp_ok, n + 1)
                if n == 0:
                    act.wait_ge(par_in, 16)
                if n >= 2:
                    act.wait_ge(k_mm, n - 1)
                act.activation(xn[:, n % 2, :].rearrange("d (p j) -> d j p", j=J),
                               psT[:, :].rearrange("d (j p) -> d j p", j=J), ACT.Identity,
                               bias=par[:, P_LNB + l:P_LNB + l + 1], scale=par[:, P_LNW + l:P_LNW + l + 1]
                               ).then_inc(xn_ok, 1)

            def evac_vr(n):
                act.wait_ge(v_mm, n + 1)
                if n >= 2:
                    act.wait_ge(kv_ok, n - 1)
                act.activation(vs[:, n % 2, :], psV[:, :], ACT.Copy, scale=0.5 * (1.0 - DECAY)).then_inc(vs_ok, 1)
                act.wait_ge(r_mm, n + 1)
                if n >= 2:
                    act.wait_ge(y_ok, n - 1)
                act.activation(th[:, n % 2, :], psR[:, :], ACT.Tanh, scale=0.5).then_inc(th_ok, 1)

            def post_x1t(q):
                act.wait_ge(x1_tp, q + 1)
                if q >= 2:
                    act.wait_ge(lin_ok, 2 * q - 2)
                act.activation(x1t[:, q % 2, :], psT[:, :], ACT.Copy).then_inc(x1t_ok, 1)

            def post_yt(q):
                if q == 0:
                    act.wait_ge(bias_ok, 1)
                if q >= 2:
                    act.wait_ge(logit_ok, q - 1)
                for b2 in range(2):
                    act.wait_ge(lin_ok, 2 * q + b2 + 1)
                    part = [t.rearrange("d (j b f) -> d b j f", j=J, b=2)[:, b2]
                            for t in (yt[:, q % 2, :], (psY, psO)[b2][:, :])]
                    last = act.activation(part[0], part[1], ACT.Identity, bias=bias[:, 2 * q + b2:2 * q + b2 + 1])
                last.then_inc(yt_ok, 1)

            def post_rows(q):
                act.wait_ge(yrow_tp, q + 1)
                act.activation(rows[:, q, :, 0:D], psX[:, :].rearrange("p (j d) -> p j d", j=J), ACT.Copy
                               ).then_inc(yrow_ok, 1)

            def post_exp(q):
                act.wait_ge(ldif_ok, q + 1)
                act.activation(lexp[:, q, :, :], ldif[:, q, :, :], ACT.Exp).then_inc(lexp_ok, 1)

            for t in range(TURNS):
                if 0 <= t - 8 < Q:
                    post_rows(t - 8)
                if t < NSTEP:
                    normalize(t)
                if 0 <= t - 1 < NSTEP:
                    evac_vr(t - 1)
                if 0 <= t - 7 < Q:
                    post_x1t(t - 7)
                    post_yt(t - 7)
                if 0 <= t - 8 < Q:
                    post_exp(t - 8)
                if t < NSTEP:
                    evac_xn(t)

            def gather_t(i):
                act.wait_ge(g_tp, i + 1)
                if i >= 2:
                    act.wait_ge(hid_mm, 2 * FC * (i - 1))
                act.activation(gt[:, i % 2, 0:512], bank[0][:, :], ACT.Copy).then_inc(gt_a, 1)

            def relu(e, parts=None):
                for n in parts or hid_parts(e)[0::2]:
                    act.wait_ge(hid_mm, n + 1)
                    if e >= 2:
                        act.wait_ge(out_mm, e - 1)
                    act.activation(hid[:, e % 2, n % FC, :], bank[2 + n % 3][:, 0:CAP], ACT.Relu,
                                   bias=par[:, P_B1 + n:P_B1 + n + 1]).then_inc(hid_a, 1)

            def out_t(e):
                act.wait_ge(out_mm, e + 1)
                if e >= 4:
                    act.wait_ge(o_tp, 2 * (e // 2) - 2)
                w = REM if e == E - 1 else CAP
                act.activation(ot[:, (e // 2) % 2, (e % 2) * CAP:(e % 2) * CAP + w], bank[5][:, 0:w], ACT.Identity,
                               bias=par[:, P_B2 + e:P_B2 + e + 1]).then_inc(ot_ok, 1)

            gather_t(0)
            for e in range(E - 1):
                relu(e)
                if e % 2:
                    gather_t((e + 1) // 2)
                if e >= 1:
                    out_t(e - 1)
            relu(E - 1, [FC * (E - 1)])
            out_t(E - 2)
            relu(E - 1, [FC * (E - 1) + 2])
            out_t(E - 1)

        @block.tensor
        def _(pe):
            def transposes(n):
                pe.wait_ge(nrm_v, n + 1)
                pe.wait_ge(nrm_a, n + 1)
                if n == 0:
                    pe.wait_ge(ident_ok, 1)
                else:
                    pe.wait_ge(xn_ok, n)
                if n == NSTEP - 1:
                    pe.wait_ge(x1t_ok, 1)
                for j in range(J):
                    last = pe.transpose(psT[:, j * 128:(j + 1) * 128], nrm[:, n % 2, j, :], identf[:, :])
                last.then_inc(tp_ok, 1)

            def project_vr(n):
                l = n // Q
                if n % Q == 0:
                    pe.wait_ge(wt_in[l], 16)
                pe.wait_ge(xn_ok, n + 1)
                if n >= 1:
                    pe.wait_ge(vs_ok, n)
                pe.matmul(psV[:, :], wt[:, l, 1, :], xn[:, n % 2, :], start=True, stop=True).then_inc(v_mm, 1)
                if n >= 1:
                    pe.wait_ge(th_ok, n)
                pe.matmul(psR[:, :], wt[:, l, 2, :], xn[:, n % 2, :], start=True, stop=True).then_inc(r_mm, 1)

            def project_k(n):
                l = n // Q
                if n >= 1:
                    pe.wait_ge(kv_ok, n)
                pe.matmul(psK[:, :], wt[:, l, 0, :], xn[:, n % 2, :], start=True, stop=True).then_inc(k_mm, 1)

            def mix_out(n):
                l = n // Q
                pe.wait_ge(y_ok, n + 1)
                if n >= 1:
                    pe.wait_ge(res_ok, n)
                if n > Q:
                    pe.wait_ge(yt_ok, n - Q)
                yj = y[:, n % 2, :].rearrange("d (p j) -> d j p", j=J)
                for j in range(J):
                    last = pe.matmul(psO[:, j * 128:(j + 1) * 128], yj[:, j, :], wt[:, l, 3, :], start=True, stop=True)
                last.then_inc(wo_ok, 1)

            def post_x1(q):
                pe.wait_ge(res_ok, Q + q + 1)
                if q >= 1:
                    pe.wait_ge(xn_ok, NSTEP)
                    pe.wait_ge(x1t_ok, q)
                for j in range(J):
                    last = pe.transpose(psT[:, j * 128:(j + 1) * 128], rows[:, q, j, D:2 * D], identf[:, :])
                last.then_inc(x1_tp, 1)

            def post_linear(q):
                pe.wait_ge(x1t_ok, q + 1)
                if q >= 1:
                    pe.wait_ge(yt_ok, q)
                for b2 in range(2):
                    pe.wait_ge(wcat_in[2 * q + b2], 16)
                    part = [t.rearrange("d (j b f) -> d b j f", j=J, b=2)[:, b2]
                            for t in ((psY, psO)[b2][:, :], x1t[:, q % 2, :])]
                    pe.matmul(part[0], wcat[:, 2 * q + b2, :], part[1], start=True, stop=True).then_inc(lin_ok, 1)

            def post_gate(q):
                pe.wait_ge(yt_ok, q + 1)
                if q >= 1:
                    pe.wait_ge(yrow_ok, q)
                for j in range(J):
                    last = pe.transpose(psX[:, j * 128:(j + 1) * 128], yt[:, q % 2, j * 128:(j + 1) * 128],
                                        identf[:, :])
                last.then_inc(yrow_tp, 1)
                if q == 0:
                    pe.wait_ge(wg_in, 16)
                else:
                    pe.wait_ge(ldif_ok, q)
                for j in range(J):
                    last = pe.matmul(logits[:, j, :], yt[:, q % 2, j * 128:(j + 1) * 128], wg_sb[:, :],
                                     start=True, stop=True)
                last.then_inc(logit_ok, 1)

            def post_before(q):
                if q == 0:
                    pe.wait_ge(vs_ok, NSTEP)
                    pe.wait_ge(tri_ok, 1)
                    pe.wait_ge(consts_ok, 4)
                else:
                    pe.wait_ge(sel_ok, q)
                for n in range(q * J):
                    pe.matmul(before_ps[:, :, :], onesb[:, :],
                              hot[:, n // J, n % J, :].unsqueeze(1).to_broadcast([128, J, E]),
                              start=(n == 0), stop=False)
                pe.wait_ge(hot_ok, q + 1)
                for j in range(J):
                    last = pe.matmul(before_ps[:, :, :], before[:, :],
                                     hot[:, q, j, :].unsqueeze(1).to_broadcast([128, J, E]),
                                     start=(q == 0 and j == 0), stop=(j == J - 1))
                    if j + 1 < J:
                        pe.matmul(before_ps[:, j + 1:J, :], identb[:, :],
                                  hot[:, q, j, :].unsqueeze(1).to_broadcast([128, J - 1 - j, E]),
                                  start=False, stop=False, skip_group_check=True)
                last.then_inc(before_ok, 1)

            for t in range(TURNS):
                if 0 <= t - 9 < Q:
                    post_before(t - 9)
                if 0 <= t - 3 < NSTEP:
                    mix_out(t - 3)
                if 0 <= t - 8 < Q:
                    post_gate(t - 8)
                if 0 <= t - 1 < NSTEP:
                    project_vr(t - 1)
                if 0 <= t - 7 < Q:
                    post_x1(t - 7)
                if 0 <= t - 1 < NSTEP:
                    project_k(t - 1)
                if 0 <= t - 7 < Q:
                    post_linear(t - 7)
                if t < NSTEP:
                    transposes(t)

            def gather_t(i):
                pe.wait_ge(in_got[i], 16)
                if i >= 1:
                    pe.wait_ge(gt_a, i)
                    pe.wait_ge(gt_v, i)
                for c in range(PC):
                    last = pe.transpose(bank[c // 4][:, (c % 4) * 128:(c % 4 + 1) * 128], got[:, i, c, 0:D],
                                        identf[:, :])
                last.then_inc(g_tp, 1)

            def hidden(e, parts=None):
                i = e // 2
                if e % 2 == 0:
                    pe.wait_ge(w1_in[i], 16)
                    pe.wait_ge(gt_a, i + 1)
                    pe.wait_ge(gt_v, i + 1)
                for n in parts or hid_parts(e):
                    if n >= 3:
                        pe.wait_ge(hid_v if (n - 3) % 2 else hid_a, (n - 3) // 2 + 1)
                    pe.matmul(bank[2 + n % 3][:, 0:CAP], w1_sb[:, e, (n % FC) * 128:(n % FC + 1) * 128],
                              gt[:, i % 2, (e % 2) * CAP:(e % 2 + 1) * CAP], start=True, stop=True
                              ).then_inc(hid_mm, 1)

            def outer(e, width=CAP):
                if e % 2 == 0:
                    pe.wait_ge(w2_in[e // 2], 16)
                if e >= 1:
                    pe.wait_ge(ot_ok, e)
                for n in hid_parts(e):
                    pe.wait_ge(hid_v if n % 2 else hid_a, n // 2 + 1)
                    last = pe.matmul(bank[5][:, 0:width], w2_sb[:, e, n % FC, :], hid[:, e % 2, n % FC, 0:width],
                                     start=(n % FC == 0), stop=(n % FC == FC - 1))
                last.then_inc(out_mm, 1)

            def direct(c):
                first = c * 128 - CAP
                for n in hid_parts(E - 1):
                    pe.wait_ge(hid_v if n % 2 else hid_a, n // 2 + 1)
                    last = pe.matmul(bank[c - 3][:, 0:D], hid[:, (E - 1) % 2, n % FC, first:first + 128],
                                     w2_sb[:, E - 1, n % FC, :], start=(n % FC == 0), stop=(n % FC == FC - 1))
                last.then_inc(direct_mm, 1)

            def back(e):
                i = e // 2
                pe.wait_ge(ot_ok, e + 1)
                if i >= 1:
                    pe.wait_ge(fin_ok, PC * (i - 1) + CHUNKS[e % 2][-1] + 1)
                for n, c in enumerate(CHUNKS[e % 2][:1] if e == E - 1 else CHUNKS[e % 2]):
                    last = pe.transpose(bank[6 + e % 2][:, n * 128:(n + 1) * 128],
                                        ot[:, i % 2, c * 128:(c + 1) * 128], identf[:, :])
                last.then_inc(o_tp, 1)

            for _n in range(WARM):
                pe.matmul(psY[:, :], onesb[:, :], warm[:, :], start=True, stop=True)
            gather_t(0)
            hidden(0)
            for e in range(E - 2):
                hidden(e + 1)
                if e:
                    back(e - 1)
                if e % 2 == 0:
                    gather_t(e // 2 + 1)
                outer(e)
            hidden(E - 1, hid_parts(E - 1)[:1])
            back(E - 3)
            outer(E - 2)
            hidden(E - 1, hid_parts(E - 1)[1:3])
            back(E - 2)
            hidden(E - 1, hid_parts(E - 1)[3:])
            outer(E - 1, REM)
            direct(3)
            back(E - 1)
            direct(4)

        @block.vector
        def _(dve):
            steps = {}

            def link(ins, s):
                steps[s.name] = steps.get(s.name, 0) + 1
                ins.then_inc(s, 1)
                dve.wait_ge(s, steps[s.name])

            dve.wait_ge(rot_in, 16)
            link(dve.tensor_scalar(ang[:, :], rot[:, R_DT:R_DT + Q], rot[:, R_FREQ:R_FREQ + 1], None, ALU.mult),
                 ang_step)
            link(dve.tensor_scalar(turns[:, 0, :], ang[:, :], 1.0 / TWO_PI, ROUND, ALU.mult, ALU.add), ang_step)
            link(dve.tensor_scalar(turns[:, 1, :], turns[:, 0, :], -ROUND, None, ALU.add), ang_step)
            link(dve.scalar_tensor_tensor(red[:, 0, :], turns[:, 1, :], -C1, ang[:, :], ALU.mult, ALU.add), ang_step)
            link(dve.scalar_tensor_tensor(red[:, 1, :], turns[:, 1, :], -C2, red[:, 0, :], ALU.mult, ALU.add),
                 ang_step)
            dve.tensor_scalar(red[:, 2, :], red[:, 1, :], 0.5, None, ALU.mult)
            dve.tensor_scalar(red[:, 3, :], red[:, 1, :], PI_IN, -PI_IN, ALU.min, ALU.max).then_inc(angles_ok, 1)
            dve.memset(empty[:, :], 0.0).then_inc(empty_ok, 1)
            dve.wait_ge(sin_ok, 1)
            link(dve.tensor_tensor(cosr[:, 0, :], sins[:, 0, :], sins[:, 0, :], ALU.mult), cos_step)
            link(dve.tensor_scalar(cosr[:, 1, :], cosr[:, 0, :], -2.0, 1.0, ALU.mult, ALU.add), cos_step)
            dve.wait_ge(amp_ok, 1)
            dve.tensor_tensor(asn[:, :], amp[:, :], sins[:, 1, :], ALU.mult).then_inc(rot_ok, 1)
            link(dve.tensor_tensor(ac[:, :], amp[:, :], cosr[:, 1, :], ALU.mult), cos_step)

            def rotate(q):
                half = BT // 2
                hq = h[:, q, :, :].rearrange("p j d -> p (j d)")
                dve.wait_ge(sx_ok, q + 1)
                dve.scalar_tensor_tensor(hq[:, 0:half], xt[:, q, 0:half], ac[:, q:q + 1], sx[:, q, half:BT],
                                         ALU.mult, ALU.subtract)
                dve.scalar_tensor_tensor(hq[:, half:BT], xt[:, q, half:BT], ac[:, q:q + 1], sx[:, q, 0:half],
                                         ALU.mult, ALU.add).then_inc(h_ok, 1)

            def norm_stats(n):
                q = n % Q
                if n < Q:
                    dve.wait_ge(h_ok, q + 1)
                else:
                    dve.wait_ge(res_ok, q + 1)
                for j in range(J):
                    dve.bn_stats(stats[:, n, j, :], h[:, q, j, :]).then_inc(stat_step, 1)
                for j in range(J):
                    dve.wait_ge(stat_step, J * n + j + 1)
                    dve.bn_aggr(mv[:, n, j, :], stats[:, n, j, :]).then_inc(mv_ok, 1)

            def normalize(n):
                dve.wait_ge(rstd_ok, n + 1)
                if n >= 2:
                    dve.wait_ge(tp_ok, n - 1)
                for j in range(HALF):
                    last = dve.tensor_scalar(nrm[:, n % 2, j, :], h[:, n % Q, j, :], mv[:, n, j, 0:1],
                                             rstd[:, n, j:j + 1], ALU.subtract, ALU.mult)
                last.then_inc(nrm_v, 1)

            def times(n):
                dve.wait_ge(k_mm, n + 1)
                dve.wait_ge(vs_ok, n + 1)
                dve.tensor_tensor(kv[:, n % 2, :], psK[:, :], vs[:, n % 2, :], ALU.mult).then_inc(kv_ok, 1)

            def scan(n):
                dve.wait_ge(kv_ok, n + 1)
                if n == 0:
                    dve.wait_ge(tables_ok, 2)
                dve.tensor_tensor_scan(st[:, n % 2, :], decay[:, :], kv[:, n % 2, :], 0.0, ALU.mult, ALU.add
                                       ).then_inc(st_ok, 1)

            def gate_y(n):
                dve.wait_ge(st_ok, n + 1)
                dve.wait_ge(th_ok, n + 1)
                if n >= 2:
                    dve.wait_ge(wo_ok, n - 1)
                dve.scalar_tensor_tensor(y[:, n % 2, :], th[:, n % 2, :], 1.0, st[:, n % 2, :], ALU.add, ALU.mult
                                         ).then_inc(y_ok, 1)

            def residual(n):
                q = n % Q
                dve.wait_ge(wo_ok, n + 1)
                ps = psO[:, :].rearrange("p (j d) -> p j d", j=J)
                if n < Q:
                    dve.wait_ge(nrm_a, n + 1)
                    dve.tensor_tensor(h[:, q, :, :], ps, h[:, q, :, :], ALU.add).then_inc(res_ok, 1)
                else:
                    dve.wait_ge(xh_ok, q + 1)
                    dve.tensor_tensor(rows[:, q, :, D:2 * D], ps, xh[:, q, :, :], ALU.add).then_inc(res_ok, 1)

            def tables():
                dve.memset(decay[:, :], DECAY).then_inc(tables_ok, 1)
                dve.wait_ge(tables_ok, 1)
                dve.memset(decay[:, :].rearrange("p (b t) -> p b t", b=2)[:, :, 0:1], 0.0).then_inc(tables_ok, 1)

            def category():
                dve.wait_ge(iotas_ok, 4)
                dve.wait_ge(tok_in, 16)
                dve.tensor_copy(rowf[:, :], rowi[:, :])
                dve.tensor_copy(catf[:, :, :], cati[:, :, :])
                dve.tensor_copy(rank[:, :, :], ranki[:, :, :])
                dve.tensor_copy(trash[:, :, :], trashi[:, :, :])
                link(dve.tensor_copy(idf[:, :], tok_id[:, :]), cat_step)
                dve.tensor_scalar(wrow[:, :], idf[:, :], float(D), rowf[:, 0:1], ALU.mult, ALU.add
                                  ).then_inc(wrow_ok, 1)
                link(dve.tensor_tensor(cat_hot[:, :, :], catf[:, :, :],
                                       idf[:, :].unsqueeze(2).to_broadcast([128, B, NCAT]), ALU.is_equal), cat_step)
                dve.wait_ge(par_in, 16)
                link(dve.tensor_tensor(cat_sel[:, :, :], cat_hot[:, :, :],
                                       par[:, P_BIAS:P_BIAS + NCAT].unsqueeze(1).to_broadcast([128, B, NCAT]),
                                       ALU.mult), cat_step)
                dve.tensor_reduce(bias[:, :], cat_sel[:, :, :], AX_X, ALU.add).then_inc(bias_ok, 1)

            def gate_max(q):
                dve.wait_ge(logit_ok, q + 1)
                dve.tensor_reduce(lmax[:, q, :], logits, AX_X, ALU.max).then_inc(lmax_ok, 1)

            def gate_dif(q):
                dve.wait_ge(lmax_ok, q + 1)
                dve.tensor_tensor(ldif[:, q, :, :], logits, lmax[:, q, :].unsqueeze(2).to_broadcast([128, J, E]),
                                  ALU.subtract).then_inc(ldif_ok, 1)

            def gate_key(q):
                dve.wait_ge(ldif_ok, q + 1)
                dve.scalar_tensor_tensor(key[:, q, :, :], ldif[:, q, :, :], 0.0, rank[:, :, :],
                                         ALU.is_ge, ALU.mult).then_inc(key_ok, 1)

            def gate_first(q):
                dve.wait_ge(key_ok, q + 1)
                dve.tensor_reduce(kmax[:, q, :], key[:, q, :, :], AX_X, ALU.max).then_inc(kmax_ok, 1)

            def gate_hot(q):
                dve.wait_ge(kmax_ok, q + 1)
                dve.tensor_tensor(hot[:, q, :, :], key[:, q, :, :],
                                  kmax[:, q, :].unsqueeze(2).to_broadcast([128, J, E]), ALU.is_equal
                                  ).then_inc(hot_ok, 1)
                dve.scalar_tensor_tensor(base[:, q, :], kmax[:, q, :], -float(CAP), trash[:, q, :],
                                         ALU.mult, ALU.subtract).then_inc(base_ok, 1)

            def gate_sum(q):
                dve.wait_ge(lexp_ok, q + 1)
                dve.tensor_reduce(lsum[:, q, :], lexp[:, q, :, :], AX_X, ALU.add).then_inc(lsum_ok, 1)

            def gate_value(q):
                dve.wait_ge(lsum_ok, q + 1)
                dve.reciprocal(rows[:, q, :, GATE], lsum[:, q, :]).then_inc(gate_ok, 1)

            def place_sel(q):
                dve.wait_ge(before_ok, q + 1)
                dve.wait_ge(hot_ok, q + 1)
                dve.tensor_tensor(sel[:, q, :, :], before_ps, hot[:, q, :, :], ALU.mult).then_inc(sel_ok, 1)

            def place_pos(q):
                dve.wait_ge(sel_ok, q + 1)
                dve.tensor_reduce(pos[:, q, :], sel[:, q, :, :], AX_X, ALU.add).then_inc(pos_ok, 1)

            def place_ofs(q):
                dve.wait_ge(pos_ok, q + 1)
                dve.wait_ge(base_ok, q + 1)
                dve.scalar_tensor_tensor(ofs[:, q, :], pos[:, q, :], float(SLOTS), base[:, q, :],
                                         ALU.add, ALU.add).then_inc(ofs_ok, 1)

            def place_kept(q):
                dve.wait_ge(ofs_ok, q + 1)
                dve.scalar_tensor_tensor(kept[:, q, :], pos[:, q, :], float(CAP), ofs[:, q, :],
                                         ALU.is_lt, ALU.mult).then_inc(kept_ok, 1)

            def place_slot(q):
                dve.wait_ge(kept_ok, q + 1)
                dve.tensor_tensor(slot[:, q, :], kept[:, q, :], trash[:, q, :], ALU.add).then_inc(slot_ok, 1)

            for t in range(TURNS):
                att, mixed, summed = t < NSTEP, 0 <= t - 2 < NSTEP, 0 <= t - 3 < NSTEP
                gated, placed = 0 <= t - 8 < Q, 0 <= t - 9 < Q
                if t < Q:
                    rotate(t)
                if att:
                    norm_stats(t)
                if t == 1:
                    tables()
                if t == 3:
                    category()
                if placed:
                    gate_sum(t - 9)
                    place_sel(t - 9)
                    gate_value(t - 9)
                    place_pos(t - 9)
                if summed:
                    residual(t - 3)
                if placed:
                    place_ofs(t - 9)
                if mixed:
                    times(t - 2)
                if gated:
                    gate_max(t - 8)
                if gated:
                    gate_dif(t - 8)
                if placed:
                    place_kept(t - 9)
                if mixed:
                    scan(t - 2)
                if placed:
                    place_slot(t - 9)
                if gated:
                    gate_key(t - 8)
                if att:
                    normalize(t)
                if gated:
                    gate_first(t - 8)
                    gate_hot(t - 8)
                if mixed:
                    gate_y(t - 2)

            def gather_t(i):
                dve.wait_ge(g_tp, i + 1)
                if i >= 2:
                    dve.wait_ge(hid_mm, 2 * FC * (i - 1))
                dve.tensor_copy(gt[:, i % 2, 512:2 * CAP], bank[1][:, 0:2 * CAP - 512]).then_inc(gt_v, 1)

            def relu(e, parts=None):
                for n in parts or hid_parts(e)[1::2]:
                    dve.wait_ge(hid_mm, n + 1)
                    if e >= 2:
                        dve.wait_ge(out_mm, e - 1)
                    dve.tensor_scalar(hid[:, e % 2, n % FC, :], bank[2 + n % 3][:, 0:CAP],
                                      par[:, P_B1 + n:P_B1 + n + 1], 0.0, ALU.add, ALU.max).then_inc(hid_v, 1)

            def finish_direct(c):
                dve.wait_ge(direct_mm, c - 2)
                dve.wait_ge(res_b2_ok, c - 2)
                dve.scalar_tensor_tensor(fin[:, PAIRS - 1, c, :], bank[c - 3][:, 0:D],
                                         got[:, PAIRS - 1, c, GATE:GATE + 1], res_b2[:, c - 3, :], ALU.mult, ALU.add
                                         ).then_inc(fin_ok, 1)

            def finish(e):
                i = e // 2
                dve.wait_ge(o_tp, e + 1)
                dve.wait_ge(rest_got[i], 16)
                for n, c in enumerate(CHUNKS[e % 2][:1] if e == E - 1 else CHUNKS[e % 2]):
                    dve.scalar_tensor_tensor(fin[:, i, c, :], bank[6 + e % 2][:, n * 128:(n + 1) * 128],
                                             got[:, i, c, GATE:GATE + 1], got[:, i, c, D:2 * D], ALU.mult, ALU.add
                                             ).then_inc(fin_ok, 1)

            gather_t(0)
            for e in range(E - 1):
                relu(e)
                if e % 2:
                    gather_t((e + 1) // 2)
                if e >= 2:
                    finish(e - 2)
            dve.wait_ge(b2_in, 16)
            dve.wait_ge(rest_got[PAIRS - 1], 16)
            for c in (3, 4):
                dve.scalar_tensor_tensor(res_b2[:, c - 3, :], b2row[:, :], got[:, PAIRS - 1, c, GATE:GATE + 1],
                                         got[:, PAIRS - 1, c, D:2 * D], ALU.mult, ALU.add).then_inc(res_b2_ok, 1)
            finish(E - 3)
            relu(E - 1, [FC * (E - 1) + 1])
            finish(E - 2)
            relu(E - 1, [FC * (E - 1) + 3])
            finish_direct(3)
            finish(E - 1)
            finish_direct(4)


def kernel(**inputs):
    import numpy as np
    import concourse.bacc as bacc
    from concourse.bass_utils import run_bass_kernel_spmd

    a = {k: np.asarray(v) for k, v in inputs.items()}

    def cols(v):
        return v.reshape(-1, D).T

    laid = {
        "x": a["x"].reshape(Q * 128, BT),
        "rot_par": np.concatenate([
            np.repeat(a["condB_deltat"].reshape(Q, 2).T, S // J, axis=0),
            np.tile(a["L0_cond_amplitudes"], 2)[:, None],
            np.tile(a["L0_cond_frequencies"], 2)[:, None]], axis=1),
        "itok": a["itok_B_0_15"].reshape(1, B),
        "params": np.concatenate([cols(a["L0_attn_ln_w"]), cols(a["L0_attn_ln_b"]), cols(a["L0_ffn_b1"]),
                                  cols(a["L0_ffn_b2"]), cols(a["L0_cond2_bias"])], axis=1),
        "wqkv": np.stack([a["L0_attn_Wk"], a["L0_attn_Wv"], a["L0_attn_Wr"], a["L0_attn_Wo"]],
                         axis=1).transpose(3, 0, 1, 2),
        "w_cat": a["L0_cond2_weight"].reshape(NCAT * D, D),
        "wg": a["L0_ffn_wg"],
        "w1": a["L0_ffn_w1"].transpose(1, 0, 2),
        "w2": a["L0_ffn_w2"].reshape(E, FC, D, D).transpose(2, 0, 1, 3),
        "b2_last": a["L0_ffn_b2"][E - 1:E],
    }
    nc = bacc.Bacc("TRN2", target_bir_lowering=False, num_devices=1)
    arrays, args = {}, []
    for name, v in laid.items():
        v = np.ascontiguousarray(v)
        arrays[name] = v
        args.append(nc.dram_tensor(name, v.shape, mybir.dt.from_np(v.dtype), kind="ExternalInput").ap())
    out = nc.dram_tensor("out", (NTOK, D), F32, kind="ExternalOutput").ap()
    build(nc, *args, out)
    r = run_bass_kernel_spmd(nc, [arrays], core_ids=[0])
    return r.results[0]["out"].reshape(B, S, D)
```

```python
from contextlib import ExitStack

import concourse.bass as bass
from concourse import mybir

ALU = mybir.AluOpType
ACT = mybir.ActivationFunctionType
AX_X = mybir.AxisListType.X
F32 = mybir.dt.float32
BF16 = mybir.dt.bfloat16
F32R = mybir.dt.float32r
I32 = mybir.dt.int32

B, S, D = 8, 256, 128
J = 4
Q = 4
BT = B * S // Q
NL = 2
E, DFF = 8, 512
FC = DFF // D
NCAT = 16
NTOK = B * S
CAP = int(1.25 * NTOK / E)
SLOTS = E * CAP
PAIRS = E // 2
PC = 2 * CAP // 128
GC = -(-CAP // 128)
CHUNKS = [range(CAP // 128), range(CAP // 128, PC)]
REM = 128 - CAP % 128
LAST_ORDER = [0, 1, 3, 2, 4]
ROW = 2 * D + 2
GATE, TOK = 2 * D, 2 * D + 1
NOBODY = 1 << 20
DECAY = 0.95
EPS = 1e-5
WARM_START = 25
WARM = 46
NORM_V = 1
NSTEP = Q * NL

P_LNW, P_LNB, P_B1, P_B2, P_BIAS = 0, NL, 2 * NL, 2 * NL + E * FC, 2 * NL + E * FC + E
NPAR = P_BIAS + NCAT
R_DT, R_AMP, R_FREQ = 0, Q, Q + 1
NROT = Q + 2

TWO_PI = 6.283185307179586
C1 = 6.28125
C2 = TWO_PI - C1
PI_IN = 3.1415925
ROUND = 12582912.0


def build(nc, x, rot_par, itok, params, wqkv, w_cat, wg, w1, w2, b2_last, out):
    ctx = ExitStack()
    with ctx:
        def sb(name, shape, dt=F32):
            return ctx.enter_context(nc.sbuf_tensor(name, shape, dt))

        def sem(name):
            return ctx.enter_context(nc.semaphore(name))

        slots = nc.dram_tensor("slots", (SLOTS + NTOK, ROW), F32).ap()

        room = sb("room", [128, 4 * Q * BT])

        def stream(i):
            return room[:, i * Q * BT:(i + 1) * Q * BT].rearrange("p (q t) -> p q t", q=Q)

        xt = stream(0)
        rot = sb("rot", [128, NROT])
        par = sb("par", [128, NPAR])
        tok_id = sb("tok_id", [128, B], I32)
        wt = sb("wt", [128, NL, 4, D])
        wcat = sb("wcat", [128, B, D])
        wg_sb = sb("wg_sb", [128, E])
        w1_sb = sb("w1_sb", [128, E, DFF])
        w2_sb = sb("w2_sb", [128, E, FC, D])

        b2row = sb("b2row", [128, D])

        identf = sb("identf", [128, 128])
        before = sb("before", [128, 128], BF16)
        identb = sb("identb", [128, 128], BF16)
        onesb = sb("onesb", [128, 128], BF16)
        decay = sb("decay", [128, BT])
        empty = sb("empty", [128, ROW])
        warm = sb("warm", [128, 512], BF16)
        mhalf = sb("mhalf", [128, J])
        rank = sb("rank", [128, J, E])
        ranki = sb("ranki", [128, J, E], I32)
        trashi = sb("trashi", [128, Q, J], I32)
        trash = sb("trash", [128, Q, J])
        cati = sb("cati", [128, B, NCAT], I32)
        catf = sb("catf", [128, B, NCAT])
        rowi = sb("rowi", [128, 1], I32)
        rowf = sb("rowf", [128, 1])
        idf = sb("idf", [128, B])
        wrow = sb("wrow", [128, B], I32)
        cat_hot = sb("cat_hot", [128, B, NCAT])
        cat_sel = sb("cat_sel", [128, B, NCAT])
        bias = sb("bias", [128, B])

        ang = sb("ang", [128, Q])
        turns = sb("turns", [128, 2, Q])
        red = sb("red", [128, 4, Q])
        sins = sb("sins", [128, 2, Q])
        cosr = sb("cosr", [128, 2, Q])
        amp = sb("amp", [128, Q])
        ac = sb("ac", [128, Q])
        asn = sb("asn", [128, Q])
        sx = stream(1)
        h = stream(2).rearrange("p q (j d) -> p q j d", j=J)
        xh = stream(3).rearrange("p q (j d) -> p q j d", j=J)
        stats = sb("stats", [128, NSTEP, J, 6])
        mv = sb("mv", [128, NSTEP, J, 2])
        veps = sb("veps", [128, NSTEP, J])
        rstd = sb("rstd", [128, NSTEP, J])
        nmean = sb("nmean", [128, NSTEP, J - NORM_V])
        shift = sb("shift", [128, NSTEP, J - NORM_V])
        nrm = sb("nrm", [128, 2, J, D])
        xn = sb("xn", [128, 2, BT])
        vs = sb("vs", [128, 2, BT])
        th = sb("th", [128, 2, BT])
        kv = sb("kv", [128, 2, BT])
        st = sb("st", [128, 2, BT])
        y = sb("y", [128, 2, BT])
        x1t = sb("x1t", [128, 2, BT])
        yt = sb("yt", [128, 2, BT])
        rows = sb("rows", [128, Q, J, ROW])
        lmax = sb("lmax", [128, Q, J])
        ldif = sb("ldif", [128, Q, J, E])
        lexp = sb("lexp", [128, Q, J, E])
        lsum = sb("lsum", [128, Q, J])
        key = sb("key", [128, Q, J, E])
        kmax = sb("kmax", [128, Q, J])
        hot = sb("hot", [128, Q, J, E], BF16)
        base = sb("base", [128, Q, J])
        sel = sb("sel", [128, Q, J, E])
        pos = sb("pos", [128, Q, J])
        ofs = sb("ofs", [128, Q, J])
        kept = sb("kept", [128, Q, J])
        slot = sb("slot", [128, Q, J], I32)

        got = sb("got", [128, PAIRS, PC, ROW])
        w1h = sb("w1h", [128, E, DFF], F32R)
        w1l = sb("w1l", [128, E, DFF], F32R)
        gh = sb("gh", [128, 2, 2 * CAP], F32R)
        gl = sb("gl", [128, 2, 2 * CAP], F32R)
        hid_end = 2 * FC * CAP
        ot_end = hid_end + 2 * 2 * CAP
        fin_end = ot_end + PAIRS * PC * D
        hid = room[:, 0:hid_end].rearrange("p (i f c) -> p i f c", i=2, f=FC)
        ot = room[:, hid_end:ot_end].rearrange("p (i c) -> p i c", i=2)
        res_b2 = room[:, fin_end:fin_end + 2 * D].rearrange("p (i d) -> p i d", i=2)
        fin = room[:, ot_end:fin_end].rearrange("p (i c d) -> p i c d", i=PAIRS, c=PC)

        bank = [ctx.enter_context(nc.psum_tensor(f"bank{i}", [128, 512], F32)) for i in range(8)]
        psT, psK, psV, psR, psO, psX, psY, psS = bank
        lin_ps = [t[:, BT // 2:BT].rearrange("d (j f) -> d j f", j=J) for t in (psY, psX)]
        logits = psS[:, 0:J * E].rearrange("p (j e) -> p j e", j=J)
        before_ps = psS[:, J * E:2 * J * E].rearrange("p (j e) -> p j e", j=J)

        x_in = [sem(f"x_in{q}") for q in range(Q)]
        rot_in, tok_in, par_in, wg_in = sem("rot_in"), sem("tok_in"), sem("par_in"), sem("wg_in")
        wt_in = [sem(f"wt_in{l}") for l in range(NL)]
        wcat_in = [sem(f"wcat_in{b}") for b in range(B)]
        w1_in = [sem(f"w1_in{i}") for i in range(PAIRS)]
        w2_in = [sem(f"w2_in{i}") for i in range(PAIRS)]
        slots_empty = sem("slots_empty")
        zeroed, ident_ok, tri_ok, consts_ok, iotas_ok = (sem("zeroed"), sem("ident_ok"), sem("tri_ok"),
                                                         sem("consts_ok"), sem("iotas_ok"))
        ac_ok = sem("ac_ok")
        cat_hot_ok, cat_sel_ok = sem("cat_hot_ok"), sem("cat_sel_ok")
        empty_ok, tables_ok, wrow_ok, bias_ok, cat_step = (sem("empty_ok"), sem("tables_ok"), sem("wrow_ok"),
                                                           sem("bias_ok"), sem("cat_step"))
        ang_step, angles_ok, sin_ok, cos_step, amp_ok, rot_ok = (sem("ang_step"), sem("angles_ok"), sem("sin_ok"),
                                                                 sem("cos_step"), sem("amp_ok"), sem("rot_ok"))
        sx_half, sx_ok, h_ok = sem("sx_half"), sem("sx_ok"), sem("h_ok")
        nmean_ok, shift_ok, nrm_a, nrm_v = sem("nmean_ok"), sem("shift_ok"), sem("nrm_a"), sem("nrm_v")
        stat_step, mv_ok, veps_ok, rstd_ok, tp_ok, xn_ok = (
            sem("stat_step"), sem("mv_ok"), sem("veps_ok"), sem("rstd_ok"), sem("tp_ok"), sem("xn_ok"))
        v_mm, r_mm, k_mm, vs_ok, th_ok, kv_ok, st_ok, y_ok, wo_ok, res_ok, xh_ok = (
            sem("v_mm"), sem("r_mm"), sem("k_mm"), sem("vs_ok"), sem("th_ok"), sem("kv_ok"), sem("st_ok"),
            sem("y_ok"), sem("wo_ok"), sem("res_ok"), sem("xh_ok"))
        x1_tp, x1t_ok, lin_ok, yt_ok, yrow_tp, yrow_ok, logit_ok = (
            sem("x1_tp"), sem("x1t_ok"), sem("lin_ok"), sem("yt_ok"), sem("yrow_tp"), sem("yrow_ok"), sem("logit_ok"))
        lmax_ok, ldif_ok, lexp_ok, lsum_ok, gate_ok, key_ok, kmax_ok, hot_ok = (
            sem("lmax_ok"), sem("ldif_ok"), sem("lexp_ok"), sem("lsum_ok"), sem("gate_ok"), sem("key_ok"),
            sem("kmax_ok"), sem("hot_ok"))
        base_ok, before_ok, sel_ok, pos_ok, ofs_ok, kept_ok, slot_ok = (
            sem("base_ok"), sem("before_ok"), sem("sel_ok"),
            sem("pos_ok"), sem("ofs_ok"), sem("kept_ok"), sem("slot_ok"))
        scattered, out_first = sem("scattered"), sem("out_first")
        first_got = sem("first_got")
        in_got = [sem(f"in_got{i}") for i in range(PAIRS)]
        b2_in, direct_mm, res_b2_ok = sem("b2_in"), sem("direct_mm"), sem("res_b2_ok")
        rest_got = [sem(f"rest_got{i}") for i in range(PAIRS)]
        w1h_ok, w1l_ok = sem("w1h_ok"), sem("w1l_ok")
        g_tp, gh_ok, gl_ok, hid_mm, hid_a, hid_v, out_mm, ot_ok, o_tp, fin_ok, out_done = (
            sem("g_tp"), sem("gh_ok"), sem("gl_ok"), sem("hid_mm"), sem("hid_a"), sem("hid_v"), sem("out_mm"),
            sem("ot_ok"), sem("o_tp"), sem("fin_ok"), sem("out_done"))

        x_q = x.rearrange("(q p) w -> q p w", q=Q)
        out_q = out.rearrange("(q p j) d -> q p j d", q=Q, j=J)
        slots_p = slots[0:SLOTS, :].rearrange("(i c p) w -> i p c w", c=PC, p=128)

        gather_cols = [slice(0, GC * 128), slice(GC * 128, 2 * CAP)]

        def hid_parts(e):
            return [FC * e + fc for fc in range(FC)]

        block = ctx.enter_context(nc.Block())

        @block.sync
        def _(sp):
            sp.dma_start(rot[:, :], rot_par).then_inc(rot_in, 16)
            sp.dma_start(xt[:, 0, :], x_q[0]).then_inc(x_in[0], 16)
            sp.dma_start(tok_id[:, :], itok.to_broadcast([128, B])).then_inc(tok_in, 16)
            sp.dma_start(xt[:, 1, :], x_q[1]).then_inc(x_in[1], 16)
            sp.dma_start(par[:, :], params).then_inc(par_in, 16)
            sp.dma_start(wt[:, 0, :, :], wqkv[:, 0, :, :]).then_inc(wt_in[0], 16)
            sp.dma_start(xt[:, 2, :], x_q[2]).then_inc(x_in[2], 16)
            sp.dma_start(xt[:, 3, :], x_q[3]).then_inc(x_in[3], 16)
            sp.dma_start(wt[:, 1, :, :], wqkv[:, 1, :, :]).then_inc(wt_in[1], 16)
            sp.dma_start(wg_sb[:, :], wg).then_inc(wg_in, 16)
            sp.wait_ge(empty_ok, 2)
            for i in range(PAIRS):
                sp.dma_start(slots_p[i], empty[:, :].unsqueeze(1).to_broadcast([128, PC, ROW])
                             ).then_inc(slots_empty, 16)
            for i in range(PAIRS):
                sp.dma_start(w1_sb[:, 2 * i:2 * i + 2, :], w1[:, 2 * i:2 * i + 2, :]).then_inc(w1_in[i], 16)
                sp.dma_start(w2_sb[:, 2 * i:2 * i + 2, :, :], w2[:, 2 * i:2 * i + 2, :, :]).then_inc(w2_in[i], 16)
            sp.dma_start(b2row[:, :], b2_last.to_broadcast([128, D])).then_inc(b2_in, 16)
            for q in range(Q):
                sp.wait_ge(res_ok, Q + q + 1)
                sp.dma_start(out_q[q], rows[:, q, :, D:2 * D]).then_inc(out_first, 16)
            sp.wait_ge(scattered, 16 * Q * J)
            for i in range(PAIRS):
                if i == 0:
                    sp.dma_start(got[:, i, 0:GC, 0:D], slots_p[i][:, 0:GC, 0:D]).then_inc(first_got, 16)
                    sp.dma_start(got[:, i, GC:PC, 0:D], slots_p[i][:, GC:PC, 0:D]).then_inc(in_got[i], 16)
                else:
                    sp.dma_start(got[:, i, :, 0:D], slots_p[i][:, :, 0:D]).then_inc(in_got[i], 16)
                sp.dma_start(got[:, i, :, D:ROW], slots_p[i][:, :, D:ROW]).then_inc(rest_got[i], 16)

        @block.gpsimd
        def _(pool):
            pool.memset(onesb[:, :], 1.0).then_inc(consts_ok, 1)
            pool.memset(warm[:, :], 1.0).then_inc(consts_ok, 1)
            pool.iota(rowi[:, :], pattern=[[0, 1]], base=0, channel_multiplier=1).then_inc(iotas_ok, 1)
            pool.memset(mhalf[:, :], -0.5).then_inc(consts_ok, 1)
            pool.iota(cati[:, :, :], pattern=[[0, B], [1, NCAT]], base=0, channel_multiplier=0).then_inc(iotas_ok, 1)
            pool.iota(ranki[:, :, :], pattern=[[0, J], [-1, E]], base=E, channel_multiplier=0).then_inc(iotas_ok, 1)
            pool.iota(trashi[:, :, :], pattern=[[BT, Q], [1, J]], base=SLOTS, channel_multiplier=J
                      ).then_inc(iotas_ok, 1)
            pool.wait_ge(rot_in, 16)
            pool.tensor_tensor(amp[:, :], rot[:, R_AMP:R_AMP + 1].to_broadcast([128, Q]), rot[:, R_DT:R_DT + Q],
                               ALU.pow).then_inc(amp_ok, 1)
            pool.memset(identf[:, :], 0.0).then_inc(zeroed, 1)
            pool.memset(decay[:, :], DECAY).then_inc(tables_ok, 1)
            pool.wait_ge(tables_ok, 1)
            pool.memset(decay[:, :].rearrange("p (b t) -> p b t", b=2)[:, :, 0:1], 0.0).then_inc(tables_ok, 1)
            pool.wait_ge(zeroed, 1)
            pool.affine_select(out=identf[:, :], in_=identf[:, :], compare_op=ALU.not_equal, fill=1.0, base=0,
                               pattern=[[-1, 128]], channel_multiplier=1).then_inc(ident_ok, 1)
            pool.wait_ge(empty_ok, 1)
            pool.iota(empty[:, TOK:TOK + 1].bitcast(I32), pattern=[[0, 1]], base=NOBODY, channel_multiplier=0
                      ).then_inc(empty_ok, 1)

            def power(n):
                pool.wait_ge(veps_ok, n + 1)
                if n == 0:
                    pool.wait_ge(consts_ok, 3)
                pool.tensor_tensor(rstd[:, n, :], veps[:, n, :], mhalf[:, :], ALU.pow).then_inc(rstd_ok, 1)
                pool.wait_ge(rstd_ok, n + 1)
                pool.wait_ge(nmean_ok, n + 1)
                pool.tensor_tensor(shift[:, n, :], nmean[:, n, :], rstd[:, n, NORM_V:J], ALU.mult).then_inc(shift_ok, 1)

            def gather_maps(b):
                pool.indirect_dma_start(wcat[:, b, :], None, w_cat,
                                        bass.IndirectOffsetOnAxis(ap=wrow[:, b:b + 1], axis=0)
                                        ).then_inc(wcat_in[b], 16)

            def add_x(q):
                pool.wait_ge(res_ok, q + 1)
                pool.tensor_tensor(xh[:, q, :, :], h[:, q, :, :],
                                   xt[:, q, :].rearrange("p (j d) -> p j d", j=J), ALU.add).then_inc(xh_ok, 1)

            power(0)
            pool.wait_ge(ident_ok, 1)
            for q in range(Q):
                pool.iota(rows[:, q, :, TOK].bitcast(I32), pattern=[[1, J]], base=BT * q, channel_multiplier=J
                          ).then_inc(iotas_ok, 1)
            power(1)
            pool.memset(before[:, :], 1.0).then_inc(zeroed, 1)
            pool.tensor_copy(identb[:, :], identf[:, :]).then_inc(consts_ok, 1)
            pool.wait_ge(zeroed, 2)
            pool.affine_select(out=before[:, :], in_=before[:, :], compare_op=ALU.is_gt, fill=0.0, base=0,
                               pattern=[[1, 128]], channel_multiplier=-1).then_inc(tri_ok, 1)
            power(2)
            power(3)
            pool.wait_ge(wrow_ok, 1)
            gather_maps(0)
            gather_maps(1)
            for n in range(Q, NSTEP):
                power(n)
                add_x(n - Q)
                gather_maps(n - 2)
            gather_maps(B - 2)
            gather_maps(B - 1)

            def scatter(q):
                pool.wait_ge(slot_ok, q + 1)
                pool.wait_ge(gate_ok, q + 1)
                pool.wait_ge(yrow_ok, q + 1)
                if q == 0:
                    pool.wait_ge(slots_empty, 16 * PAIRS)
                    pool.wait_ge(iotas_ok, 4 + Q)
                for j in range(J):
                    pool.indirect_dma_start(slots, bass.IndirectOffsetOnAxis(ap=slot[:, q, j:j + 1], axis=0),
                                            rows[:, q, j, :], None).then_inc(scattered, 16)

            for q in range(Q):
                scatter(q)
            pool.wait_ge(out_first, 16 * Q)
            for i in range(PAIRS):
                for n, c in enumerate(LAST_ORDER if i == PAIRS - 1 else range(PC)):
                    pool.wait_ge(fin_ok, PC * i + n + 1)
                    pool.indirect_dma_start(
                        out, bass.IndirectOffsetOnAxis(ap=got[:, i, c, TOK:TOK + 1].bitcast(I32), axis=0),
                        fin[:, i, c, :], None, bounds_check=NTOK - 1, oob_is_err=False).then_inc(out_done, 16)
            pool.wait_ge(out_done, 16 * PAIRS * PC)

        @block.scalar
        def _(act):
            act.preload_act_table(ACT.Sin)
            act.wait_ge(angles_ok, 1)
            act.activation(sins[:, :, :], red[:, 2:4, :], ACT.Sin).then_inc(sin_ok, 1)
            act.wait_ge(rot_ok, 1)
            act.wait_ge(x_in[0], 16)
            act.activation(sx[:, 0, BT // 2:BT], xt[:, 0, BT // 2:BT], ACT.Copy, scale=asn[:, 0:1]).then_inc(sx_half, 1)
            act.activation(sx[:, 0, 0:BT // 2], xt[:, 0, 0:BT // 2], ACT.Copy, scale=asn[:, 0:1]).then_inc(sx_ok, 1)
            for q in range(1, Q):
                act.wait_ge(x_in[q], 16)
                act.activation(sx[:, q, :], xt[:, q, :], ACT.Copy, scale=asn[:, q:q + 1]).then_inc(sx_ok, 1)
            act.preload_act_table(ACT.Exp)

            def normalize(n):
                act.wait_ge(shift_ok, n + 1)
                act.wait_ge(rstd_ok, n + 1)
                if n < Q:
                    act.wait_ge(h_ok, n + 1)
                else:
                    act.wait_ge(res_ok, n - Q + 1)
                if n >= 2:
                    act.wait_ge(tp_ok, n - 1)
                for j in range(NORM_V, J):
                    last = act.activation(nrm[:, n % 2, j, :], h[:, n % Q, j, :], ACT.Identity,
                                          bias=shift[:, n, j - NORM_V:j - NORM_V + 1], scale=rstd[:, n, j:j + 1])
                last.then_inc(nrm_a, 1)

            def evac_xn(n):
                l = n // Q
                act.wait_ge(tp_ok, n + 1)
                if n == 0:
                    act.wait_ge(par_in, 16)
                if n >= 2:
                    act.wait_ge(k_mm, n - 1)
                act.activation(xn[:, n % 2, :].rearrange("d (p j) -> d j p", j=J),
                               psT[:, :].rearrange("d (j p) -> d j p", j=J), ACT.Identity,
                               bias=par[:, P_LNB + l:P_LNB + l + 1], scale=par[:, P_LNW + l:P_LNW + l + 1]
                               ).then_inc(xn_ok, 1)

            def evac_v(n):
                act.wait_ge(v_mm, n + 1)
                if n >= 2:
                    act.wait_ge(kv_ok, n - 1)
                act.activation(vs[:, n % 2, :], psV[:, :], ACT.Copy, scale=0.5 * (1.0 - DECAY)).then_inc(vs_ok, 1)

            def evac_r(n):
                act.wait_ge(r_mm, n + 1)
                if n >= 2:
                    act.wait_ge(y_ok, n - 1)
                act.activation(th[:, n % 2, :], psR[:, :], ACT.Tanh, scale=0.5).then_inc(th_ok, 1)

            def post_x1t(q):
                act.wait_ge(x1_tp, q + 1)
                if q >= 2:
                    act.wait_ge(lin_ok, 2 * q - 2)
                act.activation(x1t[:, q % 2, :], psX[:, :], ACT.Copy).then_inc(x1t_ok, 1)

            def post_yt(q):
                if q == 0:
                    act.wait_ge(bias_ok, 1)
                if q >= 2:
                    act.wait_ge(logit_ok, q - 1)
                    act.wait_ge(yrow_tp, q - 1)
                for b2 in range(2):
                    act.wait_ge(lin_ok, 2 * q + b2 + 1)
                    part = yt[:, q % 2, :].rearrange("d (j b f) -> d b j f", j=J, b=2)[:, b2]
                    last = act.activation(part, lin_ps[b2], ACT.Identity, bias=bias[:, 2 * q + b2:2 * q + b2 + 1])
                last.then_inc(yt_ok, 1)

            def post_rows(q):
                act.wait_ge(yrow_tp, q + 1)
                act.activation(rows[:, q, :, 0:D], psT[:, :].rearrange("p (j d) -> p j d", j=J), ACT.Copy
                               ).then_inc(yrow_ok, 1)

            def post_exp(q):
                act.wait_ge(ldif_ok, q + 1)
                act.activation(lexp[:, q, :, :], ldif[:, q, :, :], ACT.Exp).then_inc(lexp_ok, 1)

            for t in range(NSTEP - 1):
                normalize(t)
                if t >= 1:
                    evac_v(t - 1)
                    evac_r(t - 1)
                evac_xn(t)
            post_x1t(0)
            normalize(7)
            post_yt(0)
            evac_v(6)
            evac_r(6)
            evac_xn(7)
            post_exp(0)
            evac_v(7)
            post_rows(0)
            post_x1t(1)
            evac_r(7)
            post_yt(1)
            post_rows(1)
            post_x1t(2)
            post_exp(1)
            post_yt(2)
            post_x1t(3)
            post_rows(2)
            post_exp(2)
            post_yt(3)
            post_exp(3)
            post_rows(3)

            def split_w1(e):
                if e % 2 == 0:
                    act.wait_ge(w1_in[e // 2], 16)
                act.activation(w1h[:, e, :], w1_sb[:, e, :], ACT.Copy).then_inc(w1h_ok, 1)

            def gather_t(i):
                if i >= 2:
                    act.wait_ge(hid_mm, 2 * FC * (i - 1))
                for part, cols in enumerate(gather_cols):
                    act.wait_ge(g_tp, 2 * i + part + 1)
                    act.activation(gh[:, i % 2, cols], bank[part][:, 0:cols.stop - cols.start], ACT.Copy
                                   ).then_inc(gh_ok, 1)

            def relu(e, parts=None):
                for n in parts or hid_parts(e)[0::2]:
                    act.wait_ge(hid_mm, n + 1)
                    if e >= 2:
                        act.wait_ge(out_mm, e - 1)
                    act.activation(hid[:, e % 2, n % FC, :], bank[2 + n % 3][:, 0:CAP], ACT.Relu,
                                   bias=par[:, P_B1 + n:P_B1 + n + 1]).then_inc(hid_a, 1)

            def out_t(e):
                act.wait_ge(out_mm, e + 1)
                if e >= 4:
                    act.wait_ge(o_tp, 2 * (e // 2) - 2)
                w = REM if e == E - 1 else CAP
                act.activation(ot[:, (e // 2) % 2, (e % 2) * CAP:(e % 2) * CAP + w], bank[5][:, 0:w], ACT.Identity,
                               bias=par[:, P_B2 + e:P_B2 + e + 1]).then_inc(ot_ok, 1)

            for e in range(E):
                split_w1(e)
            gather_t(0)
            for e in range(E - 1):
                relu(e)
                if e % 2:
                    gather_t((e + 1) // 2)
                if e >= 1:
                    out_t(e - 1)
            relu(E - 1, [FC * (E - 1)])
            out_t(E - 2)
            relu(E - 1, [FC * (E - 1) + 2])
            out_t(E - 1)

        @block.tensor
        def _(pe):
            def transposes(n):
                pe.wait_ge(nrm_v, n + 1)
                pe.wait_ge(nrm_a, n + 1)
                if n == 0:
                    pe.wait_ge(ident_ok, 1)
                else:
                    pe.wait_ge(xn_ok, n)
                for j in range(J):
                    last = pe.transpose(psT[:, j * 128:(j + 1) * 128], nrm[:, n % 2, j, :], identf[:, :])
                last.then_inc(tp_ok, 1)

            def project_v(n):
                l = n // Q
                if n % Q == 0:
                    pe.wait_ge(wt_in[l], 16)
                pe.wait_ge(xn_ok, n + 1)
                if n >= 1:
                    pe.wait_ge(vs_ok, n)
                pe.matmul(psV[:, :], wt[:, l, 1, :], xn[:, n % 2, :], start=True, stop=True).then_inc(v_mm, 1)

            def project_r(n):
                l = n // Q
                if n >= 1:
                    pe.wait_ge(th_ok, n)
                pe.matmul(psR[:, :], wt[:, l, 2, :], xn[:, n % 2, :], start=True, stop=True).then_inc(r_mm, 1)

            def project_k(n):
                l = n // Q
                if n >= 1:
                    pe.wait_ge(kv_ok, n)
                pe.matmul(psK[:, :], wt[:, l, 0, :], xn[:, n % 2, :], start=True, stop=True).then_inc(k_mm, 1)

            def mix_out(n):
                l = n // Q
                pe.wait_ge(y_ok, n + 1)
                if n >= 1:
                    pe.wait_ge(res_ok, n)
                yj = y[:, n % 2, :].rearrange("d (p j) -> d j p", j=J)
                for j in range(J):
                    last = pe.matmul(psO[:, j * 128:(j + 1) * 128], yj[:, j, :], wt[:, l, 3, :], start=True, stop=True)
                last.then_inc(wo_ok, 1)

            def post_x1(q):
                pe.wait_ge(res_ok, Q + q + 1)
                if q >= 1:
                    pe.wait_ge(yt_ok, q)
                for j in range(J):
                    last = pe.transpose(psX[:, j * 128:(j + 1) * 128], rows[:, q, j, D:2 * D], identf[:, :])
                last.then_inc(x1_tp, 1)

            def post_linear(q):
                pe.wait_ge(x1t_ok, q + 1)
                if q >= 1:
                    pe.wait_ge(yt_ok, q)
                for b2 in range(2):
                    pe.wait_ge(wcat_in[2 * q + b2], 16)
                    part = x1t[:, q % 2, :].rearrange("d (j b f) -> d b j f", j=J, b=2)[:, b2]
                    pe.matmul(lin_ps[b2], wcat[:, 2 * q + b2, :], part, start=True, stop=True).then_inc(lin_ok, 1)

            def post_yrow(q):
                pe.wait_ge(yt_ok, q + 1)
                if q == 0:
                    pe.wait_ge(xn_ok, NSTEP)
                else:
                    pe.wait_ge(yrow_ok, q)
                for j in range(J):
                    last = pe.transpose(psT[:, j * 128:(j + 1) * 128], yt[:, q % 2, j * 128:(j + 1) * 128],
                                        identf[:, :])
                last.then_inc(yrow_tp, 1)

            def post_gate(q):
                pe.wait_ge(yt_ok, q + 1)
                if q == 0:
                    pe.wait_ge(wg_in, 16)
                else:
                    pe.wait_ge(sel_ok, q)
                for j in range(J):
                    last = pe.matmul(logits[:, j, :], yt[:, q % 2, j * 128:(j + 1) * 128], wg_sb[:, :],
                                     start=True, stop=True)
                last.then_inc(logit_ok, 1)

            def keep_warm(count):
                for _n in range(count):
                    pe.matmul(psK[:, :], onesb[:, :], warm[:, :], start=True, stop=True)

            def post_before(q):
                if q == 0:
                    pe.wait_ge(tri_ok, 1)
                    pe.wait_ge(consts_ok, 4)
                pe.wait_ge(ldif_ok, q + 1)
                for n in range(q * J):
                    pe.matmul(before_ps[:, :, :], onesb[:, :],
                              hot[:, n // J, n % J, :].unsqueeze(1).to_broadcast([128, J, E]),
                              start=(n == 0), stop=False)
                pe.wait_ge(hot_ok, q + 1)
                for j in range(J):
                    last = pe.matmul(before_ps[:, :, :], before[:, :],
                                     hot[:, q, j, :].unsqueeze(1).to_broadcast([128, J, E]),
                                     start=(q == 0 and j == 0), stop=(j == J - 1))
                    if j + 1 < J:
                        pe.matmul(before_ps[:, j + 1:J, :], identb[:, :],
                                  hot[:, q, j, :].unsqueeze(1).to_broadcast([128, J - 1 - j, E]),
                                  start=False, stop=False, skip_group_check=True)
                last.then_inc(before_ok, 1)

            pe.wait_ge(consts_ok, 2)
            keep_warm(WARM_START)
            for t in range(NSTEP - 1):
                if t >= 3:
                    mix_out(t - 3)
                if t >= 1:
                    project_v(t - 1)
                    project_r(t - 1)
                if 1 <= t <= Q - 1:
                    transposes(t)
                    project_k(t - 1)
                elif t >= Q:
                    project_k(t - 1)
                    transposes(t)
                else:
                    transposes(t)
            mix_out(4)
            project_v(6)
            post_x1(0)
            project_r(6)
            post_linear(0)
            project_k(6)
            transposes(7)
            post_gate(0)
            mix_out(5)
            project_v(7)
            post_before(0)
            post_yrow(0)
            post_x1(1)
            project_r(7)
            project_k(7)
            post_linear(1)
            mix_out(6)
            post_gate(1)
            post_yrow(1)
            post_x1(2)
            mix_out(7)
            post_before(1)
            post_linear(2)
            pe.wait_ge(kv_ok, NSTEP)
            keep_warm(3)
            post_gate(2)
            post_x1(3)
            post_yrow(2)
            post_before(2)
            post_linear(3)
            keep_warm(3)
            post_gate(3)
            post_yrow(3)
            post_before(3)

            def gather_t(i):
                if i == 0:
                    pe.wait_ge(first_got, 16)
                else:
                    pe.wait_ge(in_got[i], 16)
                    pe.wait_ge(gl_ok, 2 * i)
                for c in range(PC):
                    if i == 0 and c == GC:
                        pe.wait_ge(in_got[i], 16)
                    last = pe.transpose(bank[c // GC][:, (c % GC) * 128:(c % GC + 1) * 128], got[:, i, c, 0:D],
                                        identf[:, :])
                    if c in (GC - 1, PC - 1):
                        last.then_inc(g_tp, 1)

            def hidden(e, parts=None):
                i = e // 2
                pe.wait_ge(w1h_ok, e + 1)
                pe.wait_ge(w1l_ok, e + 1)
                pe.wait_ge(gh_ok, e + 1)
                for n in parts or hid_parts(e):
                    if n >= 3:
                        pe.wait_ge(hid_v if (n - 3) % 2 else hid_a, (n - 3) // 2 + 1)
                    rows_f = slice((n % FC) * 128, (n % FC + 1) * 128)
                    cols = slice((e % 2) * CAP, (e % 2 + 1) * CAP)
                    acc = bank[2 + n % 3][:, 0:CAP]
                    pe.matmul(acc, w1h[:, e, rows_f], gh[:, i % 2, cols], start=True, stop=False)
                    pe.matmul(acc, w1l[:, e, rows_f], gh[:, i % 2, cols], start=False, stop=False)
                    pe.wait_ge(gl_ok, e + 1)
                    pe.matmul(acc, w1h[:, e, rows_f], gl[:, i % 2, cols], start=False, stop=True).then_inc(hid_mm, 1)

            def outer(e, width=CAP):
                if e % 2 == 0:
                    pe.wait_ge(w2_in[e // 2], 16)
                if e >= 1:
                    pe.wait_ge(ot_ok, e)
                for n in hid_parts(e):
                    pe.wait_ge(hid_v if n % 2 else hid_a, n // 2 + 1)
                    last = pe.matmul(bank[5][:, 0:width], w2_sb[:, e, n % FC, :], hid[:, e % 2, n % FC, 0:width],
                                     start=(n % FC == 0), stop=(n % FC == FC - 1))
                last.then_inc(out_mm, 1)

            def direct(c):
                first = c * 128 - CAP
                for n in hid_parts(E - 1):
                    pe.wait_ge(hid_v if n % 2 else hid_a, n // 2 + 1)
                    last = pe.matmul(bank[c - 3][:, 0:D], hid[:, (E - 1) % 2, n % FC, first:first + 128],
                                     w2_sb[:, E - 1, n % FC, :], start=(n % FC == 0), stop=(n % FC == FC - 1))
                last.then_inc(direct_mm, 1)

            def back(e):
                i = e // 2
                pe.wait_ge(ot_ok, e + 1)
                if i >= 1:
                    pe.wait_ge(fin_ok, PC * (i - 1) + CHUNKS[e % 2][-1] + 1)
                for n, c in enumerate(CHUNKS[e % 2][:1] if e == E - 1 else CHUNKS[e % 2]):
                    last = pe.transpose(bank[6 + e % 2][:, n * 128:(n + 1) * 128],
                                        ot[:, i % 2, c * 128:(c + 1) * 128], identf[:, :])
                last.then_inc(o_tp, 1)

            keep_warm(WARM)
            gather_t(0)
            hidden(0)
            for e in range(E - 2):
                hidden(e + 1)
                if e:
                    back(e - 1)
                if e % 2 == 0:
                    gather_t(e // 2 + 1)
                outer(e)
            hidden(E - 1, hid_parts(E - 1)[:1])
            back(E - 3)
            outer(E - 2)
            hidden(E - 1, hid_parts(E - 1)[1:3])
            back(E - 2)
            hidden(E - 1, hid_parts(E - 1)[3:])
            outer(E - 1, REM)
            direct(3)
            back(E - 1)
            direct(4)

        @block.vector
        def _(dve):
            steps = {}

            def link(ins, s):
                steps[s.name] = steps.get(s.name, 0) + 1
                ins.then_inc(s, 1)
                dve.wait_ge(s, steps[s.name])

            dve.memset(empty[:, :], 0.0).then_inc(empty_ok, 1)
            dve.wait_ge(rot_in, 16)
            link(dve.tensor_scalar(ang[:, :], rot[:, R_DT:R_DT + Q], rot[:, R_FREQ:R_FREQ + 1], None, ALU.mult),
                 ang_step)
            link(dve.tensor_scalar(turns[:, 0, :], ang[:, :], 1.0 / TWO_PI, ROUND, ALU.mult, ALU.add), ang_step)
            link(dve.tensor_scalar(turns[:, 1, :], turns[:, 0, :], -ROUND, None, ALU.add), ang_step)
            link(dve.scalar_tensor_tensor(red[:, 0, :], turns[:, 1, :], -C1, ang[:, :], ALU.mult, ALU.add), ang_step)
            link(dve.scalar_tensor_tensor(red[:, 1, :], turns[:, 1, :], -C2, red[:, 0, :], ALU.mult, ALU.add),
                 ang_step)
            dve.tensor_scalar(red[:, 2, :], red[:, 1, :], 0.5, None, ALU.mult)
            dve.tensor_scalar(red[:, 3, :], red[:, 1, :], PI_IN, -PI_IN, ALU.min, ALU.max).then_inc(angles_ok, 1)
            dve.wait_ge(sin_ok, 1)
            dve.wait_ge(amp_ok, 1)
            dve.tensor_tensor(asn[:, :], amp[:, :], sins[:, 1, :], ALU.mult).then_inc(rot_ok, 1)
            link(dve.tensor_tensor(cosr[:, 0, :], sins[:, 0, :], sins[:, 0, :], ALU.mult), cos_step)
            link(dve.tensor_scalar(cosr[:, 1, :], cosr[:, 0, :], -2.0, 1.0, ALU.mult, ALU.add), cos_step)
            dve.tensor_tensor(ac[:, :], amp[:, :], cosr[:, 1, :], ALU.mult).then_inc(ac_ok, 1)
            dve.wait_ge(iotas_ok, 4)
            dve.tensor_copy(rowf[:, :], rowi[:, :])
            dve.tensor_copy(catf[:, :, :], cati[:, :, :])
            dve.tensor_copy(rank[:, :, :], ranki[:, :, :])
            link(dve.tensor_copy(trash[:, :, :], trashi[:, :, :]), cat_step)
            dve.wait_ge(ac_ok, 1)

            def rotate(q):
                half = BT // 2
                hq = h[:, q, :, :].rearrange("p j d -> p (j d)")
                if q == 0:
                    dve.wait_ge(sx_half, 1)
                else:
                    dve.wait_ge(sx_ok, q + 1)
                dve.scalar_tensor_tensor(hq[:, 0:half], xt[:, q, 0:half], ac[:, q:q + 1], sx[:, q, half:BT],
                                         ALU.mult, ALU.subtract)
                dve.wait_ge(sx_ok, q + 1)
                dve.scalar_tensor_tensor(hq[:, half:BT], xt[:, q, half:BT], ac[:, q:q + 1], sx[:, q, 0:half],
                                         ALU.mult, ALU.add).then_inc(h_ok, 1)

            def norm_stats(n):
                q = n % Q
                if n < Q:
                    dve.wait_ge(h_ok, q + 1)
                else:
                    dve.wait_ge(res_ok, q + 1)
                for j in range(J):
                    dve.bn_stats(stats[:, n, j, :], h[:, q, j, :]).then_inc(stat_step, 1)
                for j in range(J):
                    dve.wait_ge(stat_step, J * n + j + 1)
                    dve.bn_aggr(mv[:, n, j, :], stats[:, n, j, :]).then_inc(mv_ok, 1)
                dve.wait_ge(mv_ok, J * (n + 1))
                dve.tensor_scalar(veps[:, n, :], mv[:, n, :, 1], EPS, None, ALU.add).then_inc(veps_ok, 1)
                dve.tensor_scalar(nmean[:, n, :], mv[:, n, NORM_V:J, 0], -1.0, None, ALU.mult).then_inc(nmean_ok, 1)

            def normalize(n):
                dve.wait_ge(rstd_ok, n + 1)
                if n >= 2:
                    dve.wait_ge(tp_ok, n - 1)
                for j in range(NORM_V):
                    last = dve.tensor_scalar(nrm[:, n % 2, j, :], h[:, n % Q, j, :], mv[:, n, j, 0:1],
                                             rstd[:, n, j:j + 1], ALU.subtract, ALU.mult)
                last.then_inc(nrm_v, 1)

            def times(n):
                dve.wait_ge(k_mm, n + 1)
                dve.wait_ge(vs_ok, n + 1)
                dve.tensor_tensor(kv[:, n % 2, :], psK[:, :], vs[:, n % 2, :], ALU.mult).then_inc(kv_ok, 1)

            def scan(n):
                dve.wait_ge(kv_ok, n + 1)
                if n == 0:
                    dve.wait_ge(tables_ok, 2)
                dve.tensor_tensor_scan(st[:, n % 2, :], decay[:, :], kv[:, n % 2, :], 0.0, ALU.mult, ALU.add
                                       ).then_inc(st_ok, 1)

            def gate_y(n):
                dve.wait_ge(st_ok, n + 1)
                dve.wait_ge(th_ok, n + 1)
                if n >= 2:
                    dve.wait_ge(wo_ok, n - 1)
                dve.scalar_tensor_tensor(y[:, n % 2, :], th[:, n % 2, :], 1.0, st[:, n % 2, :], ALU.add, ALU.mult
                                         ).then_inc(y_ok, 1)

            def residual(n):
                q = n % Q
                dve.wait_ge(wo_ok, n + 1)
                ps = psO[:, :].rearrange("p (j d) -> p j d", j=J)
                if n < Q:
                    dve.wait_ge(nrm_a, n + 1)
                    dve.tensor_tensor(h[:, q, :, :], ps, h[:, q, :, :], ALU.add).then_inc(res_ok, 1)
                else:
                    dve.wait_ge(xh_ok, q + 1)
                    dve.tensor_tensor(rows[:, q, :, D:2 * D], ps, xh[:, q, :, :], ALU.add).then_inc(res_ok, 1)

            def category_rows():
                dve.wait_ge(tok_in, 16)
                link(dve.tensor_copy(idf[:, :], tok_id[:, :]), cat_step)
                dve.tensor_scalar(wrow[:, :], idf[:, :], float(D), rowf[:, 0:1], ALU.mult, ALU.add
                                  ).then_inc(wrow_ok, 1)

            def category_hot():
                dve.tensor_tensor(cat_hot[:, :, :], catf[:, :, :],
                                  idf[:, :].unsqueeze(2).to_broadcast([128, B, NCAT]), ALU.is_equal
                                  ).then_inc(cat_hot_ok, 1)

            def category_sel():
                dve.wait_ge(cat_hot_ok, 1)
                dve.wait_ge(par_in, 16)
                dve.tensor_tensor(cat_sel[:, :, :], cat_hot[:, :, :],
                                  par[:, P_BIAS:P_BIAS + NCAT].unsqueeze(1).to_broadcast([128, B, NCAT]), ALU.mult
                                  ).then_inc(cat_sel_ok, 1)

            def category_bias():
                dve.wait_ge(cat_sel_ok, 1)
                dve.tensor_reduce(bias[:, :], cat_sel[:, :, :], AX_X, ALU.add).then_inc(bias_ok, 1)

            def gate_max(q):
                dve.wait_ge(logit_ok, q + 1)
                dve.tensor_reduce(lmax[:, q, :], logits, AX_X, ALU.max).then_inc(lmax_ok, 1)

            def gate_dif(q):
                dve.wait_ge(lmax_ok, q + 1)
                dve.tensor_tensor(ldif[:, q, :, :], logits, lmax[:, q, :].unsqueeze(2).to_broadcast([128, J, E]),
                                  ALU.subtract).then_inc(ldif_ok, 1)

            def gate_key(q):
                dve.wait_ge(ldif_ok, q + 1)
                dve.scalar_tensor_tensor(key[:, q, :, :], ldif[:, q, :, :], 0.0, rank[:, :, :],
                                         ALU.is_ge, ALU.mult).then_inc(key_ok, 1)

            def gate_first(q):
                dve.wait_ge(key_ok, q + 1)
                dve.tensor_reduce(kmax[:, q, :], key[:, q, :, :], AX_X, ALU.max).then_inc(kmax_ok, 1)

            def gate_hot(q):
                dve.wait_ge(kmax_ok, q + 1)
                dve.tensor_tensor(hot[:, q, :, :], key[:, q, :, :],
                                  kmax[:, q, :].unsqueeze(2).to_broadcast([128, J, E]), ALU.is_equal
                                  ).then_inc(hot_ok, 1)
                dve.scalar_tensor_tensor(base[:, q, :], kmax[:, q, :], -float(CAP), trash[:, q, :],
                                         ALU.mult, ALU.subtract).then_inc(base_ok, 1)

            def gate_sum(q):
                dve.wait_ge(lexp_ok, q + 1)
                dve.tensor_reduce(lsum[:, q, :], lexp[:, q, :, :], AX_X, ALU.add).then_inc(lsum_ok, 1)

            def gate_value(q):
                dve.wait_ge(lsum_ok, q + 1)
                dve.reciprocal(rows[:, q, :, GATE], lsum[:, q, :]).then_inc(gate_ok, 1)

            def place_sel(q):
                dve.wait_ge(before_ok, q + 1)
                dve.wait_ge(hot_ok, q + 1)
                dve.tensor_tensor(sel[:, q, :, :], before_ps, hot[:, q, :, :], ALU.mult).then_inc(sel_ok, 1)

            def place_pos(q):
                dve.wait_ge(sel_ok, q + 1)
                dve.tensor_reduce(pos[:, q, :], sel[:, q, :, :], AX_X, ALU.add).then_inc(pos_ok, 1)

            def place_ofs(q):
                dve.wait_ge(pos_ok, q + 1)
                dve.wait_ge(base_ok, q + 1)
                dve.scalar_tensor_tensor(ofs[:, q, :], pos[:, q, :], float(SLOTS), base[:, q, :],
                                         ALU.add, ALU.add).then_inc(ofs_ok, 1)

            def place_kept(q):
                dve.wait_ge(ofs_ok, q + 1)
                dve.scalar_tensor_tensor(kept[:, q, :], pos[:, q, :], float(CAP), ofs[:, q, :],
                                         ALU.is_lt, ALU.mult).then_inc(kept_ok, 1)

            def place_slot(q):
                dve.wait_ge(kept_ok, q + 1)
                dve.tensor_tensor(slot[:, q, :], kept[:, q, :], trash[:, q, :], ALU.add).then_inc(slot_ok, 1)

            def gate_choice(q):
                gate_key(q)
                gate_first(q)
                gate_hot(q)

            def place(q):
                place_sel(q)
                gate_sum(q)
                place_pos(q)
                gate_value(q)
                place_ofs(q)
                place_kept(q)
                place_slot(q)

            rotate(0)
            norm_stats(0)
            rotate(1)
            category_rows()
            normalize(0)
            norm_stats(1)
            rotate(2)
            norm_stats(2)
            normalize(1)
            rotate(3)
            norm_stats(3)
            times(0)
            normalize(2)
            scan(0)
            category_hot()
            gate_y(0)
            category_sel()
            normalize(3)
            category_bias()
            times(1)
            for t in range(3, NSTEP):
                if t >= Q:
                    norm_stats(t)
                if t == Q:
                    times(t - 2)
                residual(t - 3)
                if t > Q:
                    times(t - 2)
                scan(t - 2)
                if t >= Q:
                    normalize(t)
                gate_y(t - 2)
            times(6)
            gate_max(0)
            scan(6)
            gate_dif(0)
            gate_choice(0)
            residual(5)
            place(0)
            gate_y(6)
            times(7)
            scan(7)
            gate_y(7)
            residual(6)
            gate_max(1)
            gate_dif(1)
            gate_choice(1)
            place(1)
            residual(7)
            gate_max(2)
            gate_dif(2)
            gate_choice(2)
            place(2)
            gate_max(3)
            gate_dif(3)
            gate_choice(3)
            place(3)

            def split_w1(e):
                dve.wait_ge(w1h_ok, e + 1)
                dve.tensor_tensor(w1l[:, e, :], w1_sb[:, e, :], w1h[:, e, :], ALU.subtract).then_inc(w1l_ok, 1)

            def gather_t(i):
                if i >= 2:
                    dve.wait_ge(hid_mm, 2 * FC * (i - 1))
                for part, cols in enumerate(gather_cols):
                    dve.wait_ge(gh_ok, 2 * i + part + 1)
                    dve.tensor_tensor(gl[:, i % 2, cols], bank[part][:, 0:cols.stop - cols.start], gh[:, i % 2, cols],
                                      ALU.subtract).then_inc(gl_ok, 1)

            def relu(e, parts=None):
                for n in parts or hid_parts(e)[1::2]:
                    dve.wait_ge(hid_mm, n + 1)
                    if e >= 2:
                        dve.wait_ge(out_mm, e - 1)
                    dve.tensor_scalar(hid[:, e % 2, n % FC, :], bank[2 + n % 3][:, 0:CAP],
                                      par[:, P_B1 + n:P_B1 + n + 1], 0.0, ALU.add, ALU.max).then_inc(hid_v, 1)

            def finish_direct(c):
                dve.wait_ge(direct_mm, c - 2)
                dve.wait_ge(res_b2_ok, c - 2)
                dve.scalar_tensor_tensor(fin[:, PAIRS - 1, c, :], bank[c - 3][:, 0:D],
                                         got[:, PAIRS - 1, c, GATE:GATE + 1], res_b2[:, c - 3, :], ALU.mult, ALU.add
                                         ).then_inc(fin_ok, 1)

            def finish(e):
                i = e // 2
                dve.wait_ge(o_tp, e + 1)
                dve.wait_ge(rest_got[i], 16)
                for n, c in enumerate(CHUNKS[e % 2][:1] if e == E - 1 else CHUNKS[e % 2]):
                    dve.scalar_tensor_tensor(fin[:, i, c, :], bank[6 + e % 2][:, n * 128:(n + 1) * 128],
                                             got[:, i, c, GATE:GATE + 1], got[:, i, c, D:2 * D], ALU.mult, ALU.add
                                             ).then_inc(fin_ok, 1)

            for e in range(E):
                split_w1(e)
            gather_t(0)
            for e in range(E - 1):
                relu(e)
                if e % 2:
                    gather_t((e + 1) // 2)
                if e >= 2:
                    finish(e - 2)
            dve.wait_ge(b2_in, 16)
            dve.wait_ge(rest_got[PAIRS - 1], 16)
            for c in (3, 4):
                dve.scalar_tensor_tensor(res_b2[:, c - 3, :], b2row[:, :], got[:, PAIRS - 1, c, GATE:GATE + 1],
                                         got[:, PAIRS - 1, c, D:2 * D], ALU.mult, ALU.add).then_inc(res_b2_ok, 1)
            finish(E - 3)
            relu(E - 1, [FC * (E - 1) + 1])
            finish(E - 2)
            relu(E - 1, [FC * (E - 1) + 3])
            finish_direct(3)
            finish(E - 1)
            finish_direct(4)


def kernel(**inputs):
    import numpy as np
    import concourse.bacc as bacc
    from concourse.bass_utils import run_bass_kernel_spmd

    a = {k: np.asarray(v) for k, v in inputs.items()}

    def cols(v):
        return v.reshape(-1, D).T

    laid = {
        "x": a["x"].reshape(Q * 128, BT),
        "rot_par": np.concatenate([
            np.repeat(a["condB_deltat"].reshape(Q, 2).T, S // J, axis=0),
            np.tile(a["L0_cond_amplitudes"], 2)[:, None],
            np.tile(a["L0_cond_frequencies"], 2)[:, None]], axis=1),
        "itok": a["itok_B_0_15"].reshape(1, B),
        "params": np.concatenate([cols(a["L0_attn_ln_w"]), cols(a["L0_attn_ln_b"]), cols(a["L0_ffn_b1"]),
                                  cols(a["L0_ffn_b2"]), cols(a["L0_cond2_bias"])], axis=1),
        "wqkv": np.stack([a["L0_attn_Wk"], a["L0_attn_Wv"], a["L0_attn_Wr"], a["L0_attn_Wo"]],
                         axis=1).transpose(3, 0, 1, 2),
        "w_cat": a["L0_cond2_weight"].reshape(NCAT * D, D),
        "wg": a["L0_ffn_wg"],
        "w1": a["L0_ffn_w1"].transpose(1, 0, 2),
        "w2": a["L0_ffn_w2"].reshape(E, FC, D, D).transpose(2, 0, 1, 3),
        "b2_last": a["L0_ffn_b2"][E - 1:E],
    }
    nc = bacc.Bacc("TRN2", target_bir_lowering=False, num_devices=1)
    arrays, args = {}, []
    for name, v in laid.items():
        v = np.ascontiguousarray(v)
        arrays[name] = v
        args.append(nc.dram_tensor(name, v.shape, mybir.dt.from_np(v.dtype), kind="ExternalInput").ap())
    out = nc.dram_tensor("out", (NTOK, D), F32, kind="ExternalOutput").ap()
    build(nc, *args, out)
    r = run_bass_kernel_spmd(nc, [arrays], core_ids=[0])
    return r.results[0]["out"].reshape(B, S, D)
```
